# Optimizing a Trainium2 kernel written in Bass

```python
import numpy as np
import jax
import jax.numpy as jnp

def _softmax(x, axis=-1):
    return jax.nn.softmax(x, axis=axis)

def _gelu(x):
    return jax.nn.gelu(x, approximate=True)

def _silu(x):
    return jax.nn.silu(x)

def _sigmoid(x):
    return jax.nn.sigmoid(x)

def _layernorm(x, axis=-1, eps=1e-05):
    m = jnp.mean(x, axis=axis, keepdims=True)
    v = jnp.var(x, axis=axis, keepdims=True)
    return (x - m) / jnp.sqrt(v + eps)

def _scatter_add(tgt, idx, src, axis=0):
    return tgt.at[idx].add(src)

def _segment_sum(src, seg, n):
    return jax.ops.segment_sum(src, seg, n)
kernel_name = 'mk_seq_preln_d1_jaxref_r8_23317b'

def setup_inputs(seed: int=0):
    np.random.seed(seed)
    _w = jnp.asarray

    def _L0_attn_setup():
        import jax, jax.numpy as jnp
        import numpy as np
        B_ = 2
        S_ = 256
        H_ = 256
        NH = 16
        HD = H_ // NH
        BS = 32
        SCALE = 1.0 / np.sqrt(HD).astype(np.float32)

        def _split_heads(x):
            b, s, _ = x.shape
            return x.reshape(b, s, NH, HD).transpose(0, 2, 1, 3)

        def _attn(q, k, v):
            b, h, s, d = q.shape
            nb = s // BS
            kb = k.reshape(b, h, nb, BS, d)
            vb = v.reshape(b, h, nb, BS, d)
            scores = jnp.einsum('bhsd,bhjkd->bhsjk', q, kb) * SCALE
            qi = jnp.arange(s)
            bi = qi // BS
            bj = jnp.arange(nb)
            kidx = bj[:, None] * BS + jnp.arange(BS)[None, :]
            diag_mask = (bi[:, None, None] == bj[None, :, None]) & (kidx[None] > qi[:, None, None])
            scores = jnp.where(diag_mask[None, None], -jnp.inf, scores)
            w = jax.nn.softmax(scores.astype(jnp.float32), axis=-1)
            include = (bj[None, :] <= bi[:, None]).astype(w.dtype)
            w = w * include[None, None, :, :, None]
            out = jnp.einsum('bhsjk,bhjkd->bhsd', w, vb)
            norm = jnp.sum(w, axis=(-2, -1), keepdims=False)[..., None]
            return out / (norm + 1e-06)
        key = jax.random.key(seed)
        ks = jax.random.split(key, 5)
        return {'hidden_states': jax.random.normal(ks[0], (B_, S_, H_), dtype=jnp.float32), 'Wq': jax.random.normal(ks[1], (H_, H_), dtype=jnp.float32) * 0.02, 'Wk': jax.random.normal(ks[2], (H_, H_), dtype=jnp.float32) * 0.02, 'Wv': jax.random.normal(ks[3], (H_, H_), dtype=jnp.float32) * 0.02, 'Wo': jax.random.normal(ks[4], (H_, H_), dtype=jnp.float32) * 0.02}
    _L0_attn_in = _L0_attn_setup()

    def _L0_ffn_setup():
        import jax, jax.numpy as jnp
        import numpy as np
        NUM_EXPERTS = 8
        TOP_K = 2
        MODEL_DIM = 256
        INTER_DIM = 128
        GATE_SCALE = 1.0
        UP_SCALE = 0.0
        key = jax.random.key(seed)
        k1, k2, k3, k4 = jax.random.split(key, 4)
        hidden_states = jax.random.normal(k1, (2, 256, MODEL_DIM), jnp.float32)
        router_gate = jax.random.normal(k2, (NUM_EXPERTS, MODEL_DIM), jnp.float32) * 0.02
        expert_gate_up = jax.random.normal(k3, (NUM_EXPERTS, MODEL_DIM, 2 * INTER_DIM), jnp.float32) * 0.02
        expert_down = jax.random.normal(k4, (NUM_EXPERTS, INTER_DIM, MODEL_DIM), jnp.float32) * 0.02
        return {'hidden_states': hidden_states, 'router_gate': router_gate, 'expert_gate_up': expert_gate_up, 'expert_down': expert_down}
    _L0_ffn_in = _L0_ffn_setup()
    _d = {'L0_attn_hidden_states': _L0_attn_in['hidden_states'], 'L0_attn_Wq': _L0_attn_in['Wq'], 'L0_attn_Wk': _L0_attn_in['Wk'], 'L0_attn_Wv': _L0_attn_in['Wv'], 'L0_attn_Wo': _L0_attn_in['Wo'], 'L0_ffn_router_gate': _L0_ffn_in['router_gate'], 'L0_ffn_expert_gate_up': _L0_ffn_in['expert_gate_up'], 'L0_ffn_expert_down': _L0_ffn_in['expert_down']}
    _x0 = _d['L0_attn_hidden_states']
    _d['L0_attn_hidden_states'] = jax.random.normal(jax.random.fold_in(jax.random.key(seed), 1), (8, 256, 256), dtype=_x0.dtype)
    del _x0
    return _d

def reference(L0_attn_hidden_states, L0_attn_Wq, L0_attn_Wk, L0_attn_Wv, L0_attn_Wo, L0_ffn_router_gate, L0_ffn_expert_gate_up, L0_ffn_expert_down):

    def _L0_attn_ref(hidden_states, Wq, Wk, Wv, Wo):
        import jax, jax.numpy as jnp
        import numpy as np
        B_ = 2
        S_ = 256
        H_ = 256
        NH = 16
        HD = H_ // NH
        BS = 32
        SCALE = 1.0 / np.sqrt(HD).astype(np.float32)

        def _split_heads(x):
            b, s, _ = x.shape
            return x.reshape(b, s, NH, HD).transpose(0, 2, 1, 3)

        def _attn(q, k, v):
            b, h, s, d = q.shape
            nb = s // BS
            kb = k.reshape(b, h, nb, BS, d)
            vb = v.reshape(b, h, nb, BS, d)
            scores = jnp.einsum('bhsd,bhjkd->bhsjk', q, kb) * SCALE
            qi = jnp.arange(s)
            bi = qi // BS
            bj = jnp.arange(nb)
            kidx = bj[:, None] * BS + jnp.arange(BS)[None, :]
            diag_mask = (bi[:, None, None] == bj[None, :, None]) & (kidx[None] > qi[:, None, None])
            scores = jnp.where(diag_mask[None, None], -jnp.inf, scores)
            w = jax.nn.softmax(scores.astype(jnp.float32), axis=-1)
            include = (bj[None, :] <= bi[:, None]).astype(w.dtype)
            w = w * include[None, None, :, :, None]
            out = jnp.einsum('bhsjk,bhjkd->bhsd', w, vb)
            norm = jnp.sum(w, axis=(-2, -1), keepdims=False)[..., None]
            return out / (norm + 1e-06)
        q = _split_heads(hidden_states @ Wq.T)
        k = _split_heads(hidden_states @ Wk.T)
        v = _split_heads(hidden_states @ Wv.T)
        o = _attn(q, k, v)
        b, h, s, d = o.shape
        merged = o.transpose(0, 2, 1, 3).reshape(b, s, h * d)
        return merged @ Wo.T

    def _L0_ffn_ref(hidden_states, router_gate, expert_gate_up, expert_down):
        import jax, jax.numpy as jnp
        import numpy as np
        NUM_EXPERTS = 8
        TOP_K = 2
        MODEL_DIM = 256
        INTER_DIM = 128
        GATE_SCALE = 1.0
        UP_SCALE = 0.0
        orig_shape = hidden_states.shape
        hs = hidden_states.reshape(-1, orig_shape[-1])
        T = hs.shape[0]
        logits = hs @ router_gate.T
        probs = jax.nn.softmax(logits.astype(jnp.float32), axis=-1)
        topk_scores, topk_idx = jax.lax.top_k(probs, TOP_K)
        topk_scores = topk_scores / jnp.sum(topk_scores, axis=-1, keepdims=True)
        scores_f = topk_scores.T.reshape(-1).astype(hs.dtype)
        ids_f = topk_idx.T.reshape(-1)
        order = jnp.argsort(ids_f)
        sorted_ids = ids_f[order]
        scores_sorted = scores_f[order]
        token_slots = order % T
        x = hs[token_slots]
        inter = jnp.zeros((x.shape[0], 2 * INTER_DIM), x.dtype)
        for e in range(NUM_EXPERTS):
            m = (sorted_ids == e)[:, None]
            inter = inter + jnp.where(m, x, 0) @ expert_gate_up[e]
        gate = inter[..., 0::2]
        up = inter[..., 1::2]
        h = (up + UP_SCALE) * jax.nn.silu(gate * GATE_SCALE)
        out_rows = jnp.zeros((x.shape[0], MODEL_DIM), x.dtype)
        for e in range(NUM_EXPERTS):
            m = (sorted_ids == e)[:, None]
            out_rows = out_rows + jnp.where(m, h, 0) @ expert_down[e]
        out = jnp.zeros_like(hs).at[token_slots].add(out_rows * scores_sorted[:, None])
        return out.reshape(orig_shape)
    x = L0_attn_hidden_states
    x = x + _L0_attn_ref(_layernorm(x, axis=-1), L0_attn_Wq, L0_attn_Wk, L0_attn_Wv, L0_attn_Wo)
    x = x + _L0_ffn_ref(_layernorm(x, axis=-1), L0_ffn_router_gate, L0_ffn_expert_gate_up, L0_ffn_expert_down)
    return x

_drawn_inputs = setup_inputs


def setup_inputs(seed=0):
    import zlib

    import numpy as np

    out = dict(_drawn_inputs(seed))
    spreads = {}
    factors = {'L0_attn_Wq': 8.0,
     'L0_attn_Wk': 8.0,
     'L0_attn_Wv': 3.244,
     'L0_attn_Wo': 3.295,
     'L0_ffn_router_gate': 7.638,
     'L0_ffn_expert_gate_up': 6.636,
     'L0_ffn_expert_down': 6.643}
    for name, (base, spread) in spreads.items():
        noise = np.random.default_rng([zlib.crc32(name.encode()), seed]).standard_normal(out[name].shape)
        drawn = base * np.exp(spread * noise) if base else spread * noise
        out[name] = jnp.asarray(drawn.astype(out[name].dtype))
    for name, factor in factors.items():
        out[name] = (out[name] * factor).astype(out[name].dtype)
    return out
```

```python
from contextlib import ExitStack

import concourse.bass as bass
from concourse import mybir

ALU = mybir.AluOpType
ACT = mybir.ActivationFunctionType
AX = mybir.AxisListType
F32 = mybir.dt.float32
F32R = mybir.dt.float32r
BF16 = mybir.dt.bfloat16

P = 128
NB = 8
S = 256
TT = S // P
H = 256
KT = H // P
NH = 16
HD = H // NH
BS = 32
NBLK = S // BS
BPT = P // BS
NE = 8
NI = 128
EPS = 1e-5
SCALE = 0.25
MASKED = -1.0e30

Q_PART = [0, 1, 2, 0, 1, 0]
K_PART = [0, 0, 0, 1, 1, 2]
NPART = 3
DOT_ROWS = len(Q_PART) * HD
MAX_ROWS = NBLK * NPART
STACK = DOT_ROWS + MAX_ROWS
NC_ = BPT + NBLK
SC = NC_ * BS
VW = HD + 1
PW = BPT * VW
LOOP = (3, 2)

SCHEDULE = [
    ("xload", -1, 0), ("A", 0, 0), ("oT", 2, 0), ("dn", 3, 0),
    ("A", 0, 1), ("ln", -1, 0), ("B", 1, 0), ("wo", 2, 0), ("xT", -1, 0),
    ("A", 0, 2), ("B", 1, 1), ("PV", 1, 0), ("nm", 2, 0), ("q", -1, 0),
    ("A", 0, 3), ("B", 1, 2), ("PV", 1, 1), ("k", -1, 0), ("x2T", 2, 0),
    ("A", 0, 4), ("B", 1, 3), ("PV", 1, 2), ("rt", 2, 0), ("dn", 3, 1),
    ("A", 0, 5), ("B", 1, 4), ("PV", 1, 3), ("sT", 2, 0),
    ("A", 0, 6), ("B", 1, 5), ("PV", 1, 4), ("sb", 2, 0), ("gu", 2, 0),
    ("A", 0, 7), ("B", 1, 6), ("PV", 1, 5), ("gu", 2, 1), ("hs", 2, 0), ("sb", 2, 1),
    ("B", 1, 7), ("PV", 1, 6), ("gu", 2, 2), ("hs", 2, 1), ("stack", -1, 0), ("msplit", 0, 0),
    ("PV", 1, 7), ("gu", 2, 3), ("hs", 2, 2), ("sb", 2, 2), ("gu", 2, 4), ("hs", 2, 3),
    ("mT", 0, 0), ("v", -1, 0), ("gu", 2, 5), ("hs", 2, 4), ("sb", 2, 3),
    ("gu", 2, 6), ("hs", 2, 5), ("gu", 2, 7), ("hs", 2, 6), ("hs", 2, 7), ("xres", 1, 0),
]
SHARED = ("oT", "dn", "wo", "xT", "q", "k", "x2T", "rt", "sT", "sb", "gu", "mT", "v")
PER = {"A": 8, "B": 8, "PV": 8, "dn": 2, "gu": 8, "hs": 8, "sb": 4}
SHARED_ORDER = [n for n, (s, _, _) in enumerate(SCHEDULE) if s in SHARED]
assert len(SHARED_ORDER) % 2 == 0


class Seq:

    def __init__(self, trip, base):
        self.trip, self.base = trip, base

    def times(self, n, plus=0):
        fixed = n * self.base + plus
        return fixed if self.trip is None else self.trip * (2 * n) + fixed

    def pairs(self, n, plus=0):
        fixed = n * (self.base // 2) + plus
        return fixed if self.trip is None else self.trip * n + fixed

    @property
    def parity(self):
        return self.base % 2

    def minus(self, n):
        return Seq(self.trip, self.base - n)


def wait(eng, sem, value):
    if isinstance(value, int) and value <= 0:
        return
    eng.wait_ge(sem, value)


def steps(eng):

    def one(trip, i):
        for place, (stage, lag, index) in enumerate(SCHEDULE):
            if trip is not None or 0 <= i - lag < NB:
                yield stage, Seq(trip, i - lag), index, place, Seq(trip, i)

    first, trips = LOOP
    for i in range(-1, first):
        yield from one(None, i)
    with eng.Fori(0, trips) as trip:
        yield from one(trip, first)
        yield from one(trip, first + 1)
    for i in range(first + 2 * trips, NB + 3):
        yield from one(None, i)


def bank_before(place, step):
    n, back = SHARED_ORDER.index(place), 0
    while True:
        n -= 2
        if n < 0:
            n, back = n + len(SHARED_ORDER), back + 1
        stage, lag, index = SCHEDULE[SHARED_ORDER[n]]
        b = step.minus(back + lag)
        if step.base - back < -1:
            return None
        if step.trip is not None or 0 <= b.base < NB:
            return stage, b, index


def preln_block_attention_moe(nc, x, wqkv, wo, wr, wgu, wdn, consts, selc, out, parts_d, max_d):
    with ExitStack() as ctx:

        def sb(name, shape, dt):
            return ctx.enter_context(nc.sbuf_tensor(name, shape, dt))

        def pb(name):
            return ctx.enter_context(nc.psum_tensor(name, [P, 512], F32))

        def sem(name):
            return ctx.enter_context(nc.semaphore(name))

        wqkv_h, wqkv_l = (sb(f"wqkv_{n}", [P, KT, 3 * H], F32R) for n in "hl")
        wo_h, wo_l = (sb(f"wo_{n}", [P, KT, H], F32R) for n in "hl")
        wgu_h, wgu_l = (sb(f"wgu_{n}", [P, NE, KT, 2, NI], F32R) for n in "hl")
        wdn_h, wdn_l = (sb(f"wdn_{n}", [P, NE, H], F32R) for n in "hl")
        wr_sb = sb("wr_sb", [P, KT, NE], F32)
        raw = [sb(f"raw{n}", [P, 3 * H], F32) for n in range(2)]
        cst = sb("cst", [P, 216], F32)
        ident_f = cst[:, 0:P]
        excluded = cst[:, P:P + NC_]
        norm = cst[:, P + NC_:P + NC_ + TT]
        before = cst[:, 152:216].rearrange("p (a b) -> p a b", a=NE)
        ident_b = sb("ident_b", [P, P], BF16)
        mask_a = sb("mask_a", [P, P], BF16)
        mask_b = sb("mask_b", [P, P], BF16)
        sel = sb("sel", [MAX_ROWS, NE, P], BF16)
        minus_half = sb("minus_half", [P, TT], F32)
        x_sb = sb("x_sb", [P, TT, H], F32)
        stats = [sb(f"stats{n}", [P, TT, 6], F32) for n in range(2)]
        mv = [sb(f"mv{n}", [P, TT, 2], F32) for n in range(2)]
        veps = [sb(f"veps{n}", [P, TT], F32) for n in range(2)]
        rstd = [sb(f"rstd{n}", [P, TT], F32) for n in range(2)]
        xn = sb("xn", [P, TT, H], F32)
        xt_h, xt_l = (sb(f"xt_{n}", [P, KT, S], F32R) for n in "hl")
        parts = sb("parts", [P, NPART, 2, KT, S], BF16)
        rest = [sb(f"rest{n}", [P, KT, S], F32) for n in range(2)]
        QS = [sb(f"QS{n}", [STACK, NH, S], BF16) for n in range(2)]
        KS = [sb(f"KS{n}", [STACK, NH, S], BF16) for n in range(2)]
        VB = [sb(f"VB{n}", [P, TT, NH, PW], F32) for n in range(2)]
        nmax = sb("nmax", [P, 16, NH], F32)
        mpart = sb("mpart", [P, NPART, 16 * NH], BF16)
        mrest = sb("mrest", [P, 16 * NH], F32)
        mt_sb = sb("mt_sb", [P, NPART, S], BF16)
        PT = [sb(f"PT{n}", [P, 2, SC], F32) for n in range(2)]
        lsum = sb("lsum", [P, 2, NC_], F32)
        linv = sb("linv", [P, 2, NC_], F32)
        oblk = sb("oblk", [P, 2, NC_, HD], F32)
        o_sb = sb("o_sb", [P, TT, H], F32)
        ot_h, ot_l = (sb(f"ot_{n}", [P, KT, S], F32R) for n in "hl")
        xres = sb("xres", [P, TT, H], F32)
        x1 = [sb(f"x1{n}", [P, TT, H], F32) for n in range(2)]
        xn2 = sb("xn2", [P, TT, H], F32)
        x2_h, x2_l = (sb(f"x2_{n}", [P, KT, S], F32R) for n in "hl")
        logit = sb("logit", [P, TT, NE], F32)
        lmax = sb("lmax", [P, TT], F32)
        ldiff = sb("ldiff", [P, TT, NE], F32)
        lexp = sb("lexp", [P, TT, NE], F32)
        above = sb("above", [P, TT, NE, NE], F32)
        equal = sb("equal", [P, TT, NE, NE], F32)
        tied = sb("tied", [P, TT, NE, NE], F32)
        beats = sb("beats", [P, TT, NE, NE], F32)
        rank = sb("rank", [P, TT, NE], F32)
        picked = sb("picked", [P, TT, NE], F32)
        psumm = sb("psumm", [P, TT], F32)
        pinv = sb("pinv", [P, TT], F32)
        score = sb("score", [P, TT, NE], F32)
        spart = sb("spart", [P, TT, NPART, NE], BF16)
        srest = sb("srest", [P, TT, NE], F32)
        st_sb = sb("st_sb", [MAX_ROWS, S], BF16)
        sbc = sb("sbc", [P, NE, S], F32)
        th = [sb(f"th{n}", [P, S], F32) for n in range(2)]
        gsil = [sb(f"gsil{n}", [P, S], F32) for n in range(2)]
        ups = [sb(f"ups{n}", [P, S], F32) for n in range(2)]
        hid = [sb(f"hid{n}", [P, S], F32) for n in range(2)]
        hid_h, hid_l = (sb(f"hid_{n}", [P, NE, S], F32R) for n in "hl")

        SA = [pb(f"SA{n}") for n in range(2)]
        SB = [pb(f"SB{n}") for n in range(2)]
        PO = [pb(f"PO{n}") for n in range(2)]
        X = [pb(f"X{n}") for n in range(2)]

        ready = {s: sem(f"{s}_ready") for s in SHARED}
        drained = {s: sem(f"{s}_drained") for s in SHARED}
        consts_loaded, sel_loaded, raw_loaded = sem("consts_loaded"), sem("sel_loaded"), [sem(f"raw_loaded{n}") for n in range(2)]
        hi_split, lo_split = sem("hi_split"), sem("lo_split")
        wr_loaded = sem("wr_loaded")
        consts_cast = sem("consts_cast")
        half_set = sem("half_set")
        waits_met = sem("waits_met")
        v_cleared = sem("v_cleared")
        ind_set = sem("ind_set")
        x_loaded, xres_loaded = sem("x_loaded"), sem("xres_loaded")
        stats_done = [sem(f"stats_done{n}") for n in range(2)]
        mv_done = [sem(f"mv_done{n}") for n in range(2)]
        veps_done = [sem(f"veps_done{n}") for n in range(2)]
        rstd_done = [sem(f"rstd_done{n}") for n in range(2)]
        xn_done, xn2_done, x1_done = sem("xn_done"), sem("xn2_done"), sem("x1_done")
        hi_copied = {s: sem(f"{s}_hi") for s in ("xT", "oT", "x2T", "q", "k")}
        rest_done, mid_done, low_done = sem("rest_done"), sem("mid_done"), sem("low_done")
        parts_stored = sem("parts_stored")
        stack_loaded = [sem(f"stack_loaded{n}") for n in range(2)]
        a_ready, a_max = sem("a_ready"), sem("a_max")
        m_high, m_rest, m_mid, m_low = sem("m_high"), sem("m_rest"), sem("m_mid"), sem("m_low")
        m_stored, m_loaded = sem("m_stored"), sem("m_loaded")
        b_ready, exp_done = sem("b_ready"), sem("exp_done")
        pv_ready, pv_drained = sem("pv_ready"), sem("pv_drained")
        sum_done, inv_done, o_done = sem("sum_done"), sem("inv_done"), sem("o_done")
        lmax_done, ldiff_done, lexp_done = sem("lmax_done"), sem("ldiff_done"), sem("lexp_done")
        cmp_done, tied_done, beats_done, rank_done = sem("cmp_done"), sem("tied_done"), sem("beats_done"), sem("rank_done")
        picked_done, psumm_done, pinv_done, score_done = sem("picked_done"), sem("psumm_done"), sem("pinv_done"), sem("score_done")
        s_high, s_rest, s_mid, s_low = sem("s_high"), sem("s_rest"), sem("s_mid"), sem("s_low")
        tanh_done, act_done, hid_done, hid_hi, hid_lo = sem("tanh_done"), sem("act_done"), sem("hid_done"), sem("hid_hi"), sem("hid_lo")
        out_stored = [sem(f"out_stored{n}") for n in range(2)]

        chunks = []
        for kt in range(KT):
            chunks.append((wqkv[:, kt, :], 3 * H, wqkv_h[:, kt, :], wqkv_l[:, kt, :]))
        N_QKV = len(chunks)
        chunks.append((wo.rearrange("p k n -> p (k n)"), KT * H,
                       wo_h[:, :, :].rearrange("p k n -> p (k n)"), wo_l[:, :, :].rearrange("p k n -> p (k n)")))
        N_WO = len(chunks)
        for e in range(NE):
            v = [w[:, e:e + 1].rearrange("p e k g n -> p (e k g n)") for w in (wgu, wgu_h[:, :, :, :, :], wgu_l[:, :, :, :, :])]
            chunks.append((v[0], KT * 2 * NI, v[1], v[2]))
        N_GU = len(chunks)
        for e in range(0, NE, 2):
            v = [w[:, e:e + 2].rearrange("p e n -> p (e n)") for w in (wdn, wdn_h[:, :, :], wdn_l[:, :, :])]
            chunks.append((v[0], 2 * H, v[1], v[2]))
        N_DN = len(chunks)

        x_v = x.rearrange("b (t p) h -> b p t h", p=P)
        out_v = out.rearrange("b (t p) h -> b t p h", p=P)

        block = ctx.enter_context(nc.Block())

        def stand_alone(eng):
            eng.sem_inc(waits_met, 1)

        def row(t, b):
            return t[bass.ds(b.times(1), 1)].rearrange("a p t h -> (a p) t h") if b.trip is not None else t[b.base]

        @block.sync
        def _(sp):
            def load_chunk(n):
                if n >= 2:
                    sp.wait_ge(lo_split, n - 1)
                sp.dma_start(raw[n % 2][:, 0:chunks[n][1]], chunks[n][0]).then_inc(raw_loaded[n % 2], 16)

            sp.dma_start(x_sb[:, :, :], x_v[0]).then_inc(x_loaded, 16)
            sp.sem_inc(out_stored[1], 1)
            sp.dma_start(cst[:, :], consts[:, 0:216]).then_inc(consts_loaded, 16)
            load_chunk(0)
            load_chunk(1)
            sp.dma_start(sbc[:, 0:2, :].rearrange("p a b -> p (a b)"), consts[:, 216:728]).then_inc(sel_loaded, 16)
            sp.dma_start(sbc[0:MAX_ROWS, 2:6, :].rearrange("p a b -> p (a b)"), selc).then_inc(sel_loaded, 16)
            sp.dma_start(wr_sb[:, :, :], wr).then_inc(wr_loaded, 16)
            for n in range(2, N_DN):
                load_chunk(n)

            for stage, b, k, place, step in steps(sp):
                if stage == "xload" and not (b.trip is None and b.base == 0):
                    wait(sp, xn_done, b.times(TT))
                    stand_alone(sp)
                    sp.dma_start(x_sb[:, :, :], row(x_v, b)).then_inc(x_loaded, 16)
                if stage == "xres":
                    wait(sp, x1_done, b.times(TT))
                    stand_alone(sp)
                    sp.dma_start(xres[:, :, :], row(x_v, b)).then_inc(xres_loaded, 16)
                if stage in ("q", "k"):
                    n = 0 if stage == "q" else 1
                    sp.wait_ge(low_done, b.times(2, n + 1))
                    stand_alone(sp)
                    if n == 0 and not (b.trip is None and b.base < 2):
                        wait(sp, stack_loaded[b.parity], b.pairs(16 * 12))
                        stand_alone(sp)
                    for p in range(NPART):
                        sp.dma_start(parts_d[b.parity, p, n].rearrange("(t q) s -> q t s", q=P),
                                     parts[:, p, n, :, :]).then_inc(parts_stored, 16)
                if stage == "stack":
                    sp.wait_ge(parts_stored, b.times(16 * 6, 16 * 6))
                    stand_alone(sp)
                    if not (b.trip is None and b.base < 2):
                        sp.wait_ge(b_ready, b.times(NH, -NH))
                        stand_alone(sp)
                    for r in range(len(Q_PART)):
                        for n, stk, part in ((0, QS, Q_PART[r]), (1, KS, K_PART[r])):
                            src = parts_d[b.parity, part, n].rearrange("(h d) s -> d h s", d=HD)
                            sp.dma_start(stk[b.parity][HD * r:HD * (r + 1), :, :], src)\
                                .then_inc(stack_loaded[b.parity], 16)
                if stage == "mT":
                    sp.wait_ge(drained["mT"], b.times(1, 1))
                    stand_alone(sp)
                    for p in range(NPART):
                        sp.dma_start(max_d[p].rearrange("j h s -> (j h) s"), mt_sb[:, p, :])\
                            .then_inc(m_stored, 16)
                    sp.wait_ge(m_stored, b.times(16 * NPART, 16 * NPART))
                    stand_alone(sp)
                    sp.dma_start(QS[b.parity][DOT_ROWS:STACK, :, :], max_d.rearrange("p j h s -> (p j) h s"))\
                        .then_inc(m_loaded, 16)
                if stage == "dn":
                    sp.wait_ge(drained["dn"], b.times(TT, k + 1))
                    stand_alone(sp)
                    dst = out_v[bass.ds(b.times(1), 1), k].rearrange("a p h -> (a p) h") if b.trip is not None \
                        else out_v[b.base, k]
                    sp.dma_start(dst, x1[b.parity][:, k, :]).then_inc(out_stored[b.parity], 16)
            for n in range(2):
                sp.wait_ge(out_stored[n], 16 * TT * NB // 2 + n)
                stand_alone(sp)

        @block.scalar
        def _(act):
            def split_hi(n):
                act.wait_ge(raw_loaded[n % 2], 16 * (n // 2 + 1))
                nc.scalar.copy(chunks[n][2], raw[n % 2][:, 0:chunks[n][1]]).then_inc(hi_split, 1)

            split_hi(0)
            split_hi(1)
            act.wait_ge(sel_loaded, 32)
            nc.scalar.copy(mask_a[:, :], sbc[:, 0, 0:P]).then_inc(consts_cast, 1)
            nc.scalar.copy(mask_b[:, :], sbc[:, 0, P:2 * P]).then_inc(consts_cast, 1)
            nc.scalar.copy(sel[:, :, :], sbc[0:MAX_ROWS, 2:6, :].rearrange("p a b -> p (a b)")
                           .rearrange("p (e n) -> p e n", e=NE)).then_inc(consts_cast, 1)
            act.wait_ge(consts_loaded, 16)
            nc.scalar.copy(ident_b[:, :], ident_f).then_inc(consts_cast, 1)
            for n in range(2):
                ind = sbc[DOT_ROWS:STACK, 1, :].unsqueeze(1).to_broadcast([MAX_ROWS, NH, S])
                nc.scalar.copy(KS[n][DOT_ROWS:STACK, :, :], ind).then_inc(ind_set, 1)
            for n in range(2, N_DN):
                split_hi(n)

            for stage, b, k, place, step in steps(act):
                if stage in ("xT", "oT", "x2T"):
                    bank = X[SHARED_ORDER.index(place) % 2]
                    hi = {"xT": xt_h, "oT": ot_h, "x2T": x2_h}[stage]
                    reader, n = {"xT": ("v", 1), "oT": ("wo", 1), "x2T": ("gu", NE)}[stage]
                    act.wait_ge(ready[stage], b.times(1, 1))
                    wait(act, ready[reader], b.times(n))
                    nc.scalar.copy(hi[:, :, :], bank[:, :].rearrange("p (k s) -> p k s", k=KT))\
                        .then_inc(hi_copied[stage], 1)
                if stage in ("q", "k"):
                    bank = X[SHARED_ORDER.index(place) % 2]
                    n = 0 if stage == "q" else 1
                    act.wait_ge(ready[stage], b.times(1, 1))
                    wait(act, parts_stored, b.times(16 * 6))
                    nc.scalar.copy(parts[:, 0, n, :, :], bank[:, :].rearrange("p (k s) -> p k s", k=KT))\
                        .then_inc(hi_copied[stage], 1)
                if stage == "v":
                    bank = X[SHARED_ORDER.index(place) % 2]
                    act.wait_ge(ready["v"], b.times(1, 1))
                    if b.trip is None and b.base < 2:
                        act.wait_ge(v_cleared, (BPT + 1) * (b.base + 1))
                    else:
                        act.wait_ge(pv_ready, b.times(8, -8))
                    for j in range(BPT):
                        q = slice(BS * j, BS * (j + 1))
                        dst = VB[b.parity][q, :, :, VW * j:VW * j + HD]
                        src = bank[q, :].rearrange("p (t h d) -> p t h d", t=TT, h=NH)
                        last = nc.scalar.copy(dst, src)
                    last.then_inc(drained["v"], 1)
                if stage == "mT":
                    bank = X[SHARED_ORDER.index(place) % 2][:, :].bitcast(BF16)
                    act.wait_ge(ready["mT"], b.times(1, 1))
                    wait(act, m_stored, b.times(16 * NPART))
                    nc.scalar.copy(mt_sb[:, :, :], bank[:, 0:NPART * S].rearrange("p (a s) -> p a s", a=NPART))\
                        .then_inc(drained["mT"], 1)
                if stage == "B":
                    if k >= 2 or not (b.trip is None and b.base == 0):
                        act.wait_ge(pv_ready, b.times(8, k - 1))
                    for h in (2 * k, 2 * k + 1):
                        act.wait_ge(b_ready, b.times(NH, h + 1))
                        nc.scalar.activation(PT[k % 2][:, h % 2, :], SB[h % 2][:, 0:SC], ACT.Exp, scale=SCALE)\
                            .then_inc(exp_done, 1)
                if stage == "rt":
                    act.wait_ge(ldiff_done, b.times(1, 1))
                    wait(act, picked_done, b.times(1))
                    nc.scalar.activation(lexp[:, :, :], ldiff[:, :, :], ACT.Exp).then_inc(lexp_done, 1)
                if stage == "sT":
                    bank = X[SHARED_ORDER.index(place) % 2][:, :].bitcast(BF16)
                    act.wait_ge(ready["sT"], b.times(1, 1))
                    wait(act, ready["sb"], b.times(4))
                    nc.scalar.copy(st_sb[:, :], bank[0:MAX_ROWS, 0:S]).then_inc(drained["sT"], 1)
                if stage == "sb":
                    bank = X[SHARED_ORDER.index(place) % 2]
                    act.wait_ge(ready["sb"], b.times(4, k + 1))
                    if not (b.trip is None and b.base == 0):
                        act.wait_ge(drained["gu"], b.times(NE, 2 * k + 2 - NE))
                    nc.scalar.copy(sbc[:, 2 * k:2 * k + 2, :], bank[:, :].rearrange("p (e s) -> p e s", e=2))\
                        .then_inc(drained["sb"], 1)
                if stage == "gu":
                    bank = X[SHARED_ORDER.index(place) % 2]
                    act.wait_ge(ready["gu"], b.times(NE, k + 1))
                    if k >= 2 or not (b.trip is None and b.base == 0):
                        act.wait_ge(drained["gu"], b.times(NE, k - 1))
                    nc.scalar.activation(th[k % 2][:, :], bank[:, 0:S], ACT.Tanh, scale=0.5).then_inc(tanh_done, 1)
                if stage == "hs":
                    act.wait_ge(hid_done, b.times(NE, k + 1))
                    wait(act, ready["dn"], b.times(TT))
                    nc.scalar.copy(hid_h[:, k, :], hid[k % 2][:, :]).then_inc(hid_hi, 1)

        @block.gpsimd
        def _(pool):
            nc.gpsimd.memset(minus_half[:, :], -0.5).then_inc(half_set, 1)
            nc.gpsimd.memset(nmax[:, NC_:16, :], 0.0).then_inc(half_set, 1)
            for n in range(2):
                if n:
                    pool.wait_ge(v_cleared, n * (BPT + 1))
                nc.gpsimd.memset(VB[n][:, :, :, :], 0.0).then_inc(v_cleared, 1)
                for j in range(BPT):
                    pool.wait_ge(v_cleared, n * (BPT + 1) + 1 + j)
                    nc.gpsimd.memset(VB[n][BS * j:BS * (j + 1), :, :, VW * j + HD:VW * (j + 1)], 1.0)\
                        .then_inc(v_cleared, 1)
            pool.wait_ge(half_set, 2)
            pool.wait_ge(v_cleared, 2 * (BPT + 1))

            for stage, b, k, place, step in steps(pool):
                if stage in ("ln", "wo"):
                    n = 0 if stage == "ln" else 1
                    pool.wait_ge(mv_done[n], b.times(TT, TT))
                    wait(pool, xn2_done if n else xn_done, b.times(TT))
                    stand_alone(pool)
                    nc.gpsimd.tensor_scalar(veps[n][:, :], mv[n][:, :, 1], EPS, None, ALU.add)\
                        .then_inc(veps_done[n], 1)
                    pool.wait_ge(veps_done[n], b.times(1, 1))
                    nc.gpsimd.tensor_tensor(rstd[n][:, :], veps[n][:, :], minus_half[:, :], ALU.pow)\
                        .then_inc(rstd_done[n], 1)
                if stage in ("q", "k"):
                    n = 0 if stage == "q" else 1
                    pool.wait_ge(rest_done, b.times(2, n + 1))
                    wait(pool, parts_stored, b.times(16 * 6))
                    stand_alone(pool)
                    nc.gpsimd.tensor_copy(parts[:, 1, n, :, :], rest[n][:, :, :]).then_inc(mid_done, 1)
                    pool.wait_ge(mid_done, b.times(2, n + 1))
                    nc.gpsimd.tensor_tensor(parts[:, 2, n, :, :], rest[n][:, :, :], parts[:, 1, n, :, :],
                                            ALU.subtract).then_inc(low_done, 1)
                if stage == "msplit":
                    m = nmax[:, :, :].rearrange("p c h -> p (c h)")
                    pool.wait_ge(a_max, b.times(NH, NH))
                    wait(pool, ready["mT"], b.times(1))
                    stand_alone(pool)
                    nc.gpsimd.tensor_copy(mpart[:, 0, :], m).then_inc(m_high, 1)
                    pool.wait_ge(m_high, b.times(1, 1))
                    nc.gpsimd.tensor_tensor(mrest[:, :], m, mpart[:, 0, :], ALU.subtract).then_inc(m_rest, 1)
                    pool.wait_ge(m_rest, b.times(1, 1))
                    stand_alone(pool)
                    nc.gpsimd.tensor_copy(mpart[:, 1, :], mrest[:, :]).then_inc(m_mid, 1)
                    pool.wait_ge(m_mid, b.times(1, 1))
                    nc.gpsimd.tensor_tensor(mpart[:, 2, :], mrest[:, :], mpart[:, 1, :], ALU.subtract)\
                        .then_inc(m_low, 1)
                if stage == "rt":
                    pool.wait_ge(score_done, b.times(1, 1))
                    wait(pool, ready["sT"], b.times(1))
                    stand_alone(pool)
                    nc.gpsimd.tensor_copy(spart[:, :, 0, :], score[:, :, :]).then_inc(s_high, 1)
                    pool.wait_ge(s_high, b.times(1, 1))
                    nc.gpsimd.tensor_tensor(srest[:, :, :], score[:, :, :], spart[:, :, 0, :], ALU.subtract)\
                        .then_inc(s_rest, 1)
                    pool.wait_ge(s_rest, b.times(1, 1))
                    stand_alone(pool)
                    nc.gpsimd.tensor_copy(spart[:, :, 1, :], srest[:, :, :]).then_inc(s_mid, 1)
                    pool.wait_ge(s_mid, b.times(1, 1))
                    nc.gpsimd.tensor_tensor(spart[:, :, 2, :], srest[:, :, :], spart[:, :, 1, :], ALU.subtract)\
                        .then_inc(s_low, 1)
                if stage == "gu":
                    pool.wait_ge(act_done, b.times(NE, k + 1))
                    pool.wait_ge(drained["gu"], b.times(NE, k + 1))
                    if k >= 2 or not (b.trip is None and b.base == 0):
                        pool.wait_ge(hid_hi, b.times(NE, k - 1))
                        pool.wait_ge(hid_lo, b.times(NE, k - 1))
                    nc.gpsimd.tensor_tensor(hid[k % 2][:, :], gsil[k % 2][:, :], ups[k % 2][:, :], ALU.mult)\
                        .then_inc(hid_done, 1)
                if stage == "hs":
                    pool.wait_ge(hid_hi, b.times(NE, k + 1))
                    pool.wait_ge(hid_done, b.times(NE, k + 1))
                    wait(pool, ready["dn"], b.times(TT))
                    nc.gpsimd.tensor_tensor(hid_l[:, k, :], hid[k % 2][:, :], hid_h[:, k, :].bitcast(F32),
                                            ALU.subtract).then_inc(hid_lo, 1)

        @block.vector
        def _(dve):
            def split_lo(n):
                dve.wait_ge(hi_split, n + 1)
                dve.wait_ge(raw_loaded[n % 2], 16 * (n // 2 + 1))
                nc.vector.tensor_tensor(chunks[n][3], raw[n % 2][:, 0:chunks[n][1]], chunks[n][2].bitcast(F32),
                                        ALU.subtract).then_inc(lo_split, 1)

            def layernorm_stats(n, b, src):
                for t in range(TT):
                    nc.vector.bn_stats(stats[n][:, t, :], src[:, t, :]).then_inc(stats_done[n], 1)
                for t in range(TT):
                    dve.wait_ge(stats_done[n], b.times(TT, t + 1))
                    stand_alone(dve)
                    nc.vector.bn_aggr(mv[n][:, t, :], stats[n][:, t, :]).then_inc(mv_done[n], 1)

            def normalise(n, b, dst, src, done):
                dve.wait_ge(rstd_done[n], b.times(1, 1))
                for t in range(TT):
                    nc.vector.tensor_scalar(dst[:, t, :], src[:, t, :], mv[n][:, t, 0:1], rstd[n][:, t:t + 1],
                                            ALU.subtract, ALU.mult).then_inc(done, 1)

            for stage, b, k, place, step in steps(dve):
                if stage == "ln":
                    dve.wait_ge(x_loaded, b.times(16, 16))
                    layernorm_stats(0, b, x_sb)
                    wait(dve, ready["xT"], b.times(1))
                    normalise(0, b, xn, x_sb, xn_done)
                    if b.trip is None and b.base == 0:
                        for n in range(N_DN):
                            split_lo(n)
                if stage in ("xT", "oT", "x2T"):
                    bank = X[SHARED_ORDER.index(place) % 2]
                    hi, lo = {"xT": (xt_h, xt_l), "oT": (ot_h, ot_l), "x2T": (x2_h, x2_l)}[stage]
                    reader, n = {"xT": ("v", 1), "oT": ("wo", 1), "x2T": ("gu", NE)}[stage]
                    dve.wait_ge(hi_copied[stage], b.times(1, 1))
                    wait(dve, ready[reader], b.times(n))
                    nc.vector.tensor_tensor(lo[:, :, :], bank[:, :].rearrange("p (k s) -> p k s", k=KT),
                                            hi[:, :, :].bitcast(F32), ALU.subtract).then_inc(drained[stage], 1)
                if stage in ("q", "k"):
                    bank = X[SHARED_ORDER.index(place) % 2]
                    n = 0 if stage == "q" else 1
                    dve.wait_ge(hi_copied[stage], b.times(1, 1))
                    wait(dve, low_done, b.times(2))
                    nc.vector.tensor_tensor(rest[n][:, :, :], bank[:, :].rearrange("p (k s) -> p k s", k=KT),
                                            parts[:, 0, n, :, :], ALU.subtract)\
                        .then_inc(rest_done, 1)
                if stage == "A":
                    if k == 0:
                        wait(dve, m_low, b.times(1))
                    for h in (2 * k, 2 * k + 1):
                        dve.wait_ge(a_ready, b.times(NH, h + 1))
                        nc.vector.tensor_reduce(nmax[:, 0:NC_, h], SA[h % 2][:, 0:SC]
                                                .rearrange("p (c s) -> p c s", s=BS), AX.X, ALU.max, negate=True)\
                            .then_inc(a_max, 1)
                if stage == "PV":
                    po = PO[k % 2][:, 0:2 * NC_ * VW].rearrange("p (h c v) -> p h c v", h=2, v=VW)
                    dve.wait_ge(pv_ready, b.times(8, k + 1))
                    wait(dve, inv_done, b.times(8, k))
                    nc.vector.tensor_tensor(lsum[:, :, :], po[:, :, :, HD],
                                            excluded.unsqueeze(1).to_broadcast([P, 2, NC_]), ALU.add)\
                        .then_inc(sum_done, 1)
                    dve.wait_ge(sum_done, b.times(8, k + 1))
                    wait(dve, pv_drained, b.times(8, k))
                    nc.vector.reciprocal(linv[:, :, :], lsum[:, :, :]).then_inc(inv_done, 1)
                    dve.wait_ge(inv_done, b.times(8, k + 1))
                    wait(dve, o_done, b.times(16, 2 * k))
                    for h in range(2):
                        last = nc.vector.tensor_tensor(oblk[:, h, :, :], po[:, h, :, 0:HD],
                                                linv[:, h, :].unsqueeze(2).to_broadcast([P, NC_, HD]), ALU.mult)
                    last.then_inc(pv_drained, 1)
                    dve.wait_ge(pv_drained, b.times(8, k + 1))
                    if k == 0:
                        wait(dve, ready["oT"], b.times(1))
                    for t, c in ((0, slice(NBLK, NC_)), (1, slice(0, NBLK))):
                        nc.vector.tensor_reduce(
                            o_sb[:, t, 2 * HD * k:2 * HD * (k + 1)].rearrange("p (h d) -> p h d", h=2),
                            oblk[:, :, c, :].rearrange("p h c d -> p h d c"), AX.X, ALU.add).then_inc(o_done, 1)
                if stage == "wo":
                    bank = X[SHARED_ORDER.index(place) % 2]
                    y = x1[b.parity]
                    dve.wait_ge(ready["wo"], b.times(1, 1))
                    dve.wait_ge(xres_loaded, b.times(16, 16))
                    if not (b.trip is None and b.base < 2):
                        dve.wait_ge(out_stored[b.parity], b.pairs(16 * TT, b.parity))
                    for t in range(TT):
                        nc.vector.scalar_tensor_tensor(out=y[:, t, :], in0=bank[:, H * t:H * (t + 1)],
                                                       scalar=norm[:, t:t + 1], in1=xres[:, t, :],
                                                       op0=ALU.mult, op1=ALU.add).then_inc(x1_done, 1)
                    dve.wait_ge(x1_done, b.times(TT, TT))
                    layernorm_stats(1, b, y)
                if stage == "nm":
                    wait(dve, ready["x2T"], b.times(1))
                    normalise(1, b, xn2, x1[b.parity], xn2_done)
                if stage == "rt":
                    bank = X[SHARED_ORDER.index(place) % 2]
                    dve.wait_ge(ready["rt"], b.times(1, 1))
                    nc.vector.tensor_copy(logit[:, :, :], bank[:, 0:TT * NE].rearrange("p (t e) -> p t e", t=TT))\
                        .then_inc(drained["rt"], 1)
                    dve.wait_ge(drained["rt"], b.times(1, 1))
                    nc.vector.tensor_reduce(lmax[:, :], logit[:, :, :], AX.X, ALU.max).then_inc(lmax_done, 1)
                    dve.wait_ge(lmax_done, b.times(1, 1))
                    wait(dve, lexp_done, b.times(1))
                    nc.vector.tensor_tensor(ldiff[:, :, :], logit[:, :, :],
                                            lmax[:, :].unsqueeze(2).to_broadcast([P, TT, NE]), ALU.subtract)\
                        .then_inc(ldiff_done, 1)
                    for t in range(TT):
                        mine = logit[:, t, :].unsqueeze(2).to_broadcast([P, NE, NE])
                        other = logit[:, t, :].unsqueeze(1).to_broadcast([P, NE, NE])
                        nc.vector.tensor_tensor(equal[:, t], other, mine, ALU.is_equal).then_inc(cmp_done, 1)
                        nc.vector.tensor_tensor(above[:, t], other, mine, ALU.is_gt).then_inc(cmp_done, 1)
                    dve.wait_ge(cmp_done, b.times(2 * TT, 2 * TT))
                    nc.vector.tensor_tensor(tied[:, :, :, :], equal[:, :, :, :],
                                            before.unsqueeze(1).to_broadcast([P, TT, NE, NE]), ALU.mult)\
                        .then_inc(tied_done, 1)
                    dve.wait_ge(tied_done, b.times(1, 1))
                    nc.vector.tensor_tensor(beats[:, :, :, :], tied[:, :, :, :], above[:, :, :, :], ALU.add)\
                        .then_inc(beats_done, 1)
                    dve.wait_ge(beats_done, b.times(1, 1))
                    nc.vector.tensor_reduce(rank[:, :, :], beats[:, :, :, :], AX.X, ALU.add).then_inc(rank_done, 1)
                    dve.wait_ge(rank_done, b.times(1, 1))
                    dve.wait_ge(lexp_done, b.times(1, 1))
                    nc.vector.scalar_tensor_tensor(out=picked[:, :, :], in0=rank[:, :, :], scalar=1.5,
                                                   in1=lexp[:, :, :], op0=ALU.is_lt, op1=ALU.mult)\
                        .then_inc(picked_done, 1)
                    dve.wait_ge(picked_done, b.times(1, 1))
                    nc.vector.tensor_reduce(psumm[:, :], picked[:, :, :], AX.X, ALU.add).then_inc(psumm_done, 1)
                    dve.wait_ge(psumm_done, b.times(1, 1))
                    wait(dve, s_low, b.times(1))
                    wait(dve, s_rest, b.times(1))
                    nc.vector.reciprocal(pinv[:, :], psumm[:, :]).then_inc(pinv_done, 1)
                    dve.wait_ge(pinv_done, b.times(1, 1))
                    nc.vector.tensor_tensor(score[:, :, :], picked[:, :, :],
                                            pinv[:, :].unsqueeze(2).to_broadcast([P, TT, NE]), ALU.mult)\
                        .then_inc(score_done, 1)
                if stage == "gu":
                    bank = X[SHARED_ORDER.index(place) % 2]
                    dve.wait_ge(tanh_done, b.times(NE, k + 1))
                    dve.wait_ge(drained["sb"], b.times(4, k // 2 + 1))
                    if k >= 2 or not (b.trip is None and b.base == 0):
                        dve.wait_ge(hid_done, b.times(NE, k - 1))
                    nc.vector.scalar_tensor_tensor(out=gsil[k % 2][:, :], in0=th[k % 2][:, :], scalar=1.0,
                                                   in1=bank[:, 0:S], op0=ALU.add, op1=ALU.mult).then_inc(act_done, 1)
                    last = nc.vector.scalar_tensor_tensor(out=ups[k % 2][:, :], in0=bank[:, S:2 * S], scalar=0.5,
                                                          in1=sbc[:, k, :], op0=ALU.mult, op1=ALU.mult)
                    last.then_inc(drained["gu"], 1)
                if stage == "dn":
                    bank = X[SHARED_ORDER.index(place) % 2]
                    dve.wait_ge(ready["dn"], b.times(TT, k + 1))
                    dve.wait_ge(x1_done, b.times(TT, TT))
                    nc.vector.tensor_tensor(x1[b.parity][:, k, :], bank[:, 0:H], x1[b.parity][:, k, :], ALU.add)\
                        .then_inc(drained["dn"], 1)

        @block.tensor
        def _(pe):
            def three_products(dst, lhs, rhs, ks, first, last):
                todo = [(k, p) for k in ks for p in ((0, 0), (0, 1), (1, 0))]
                for n, (k, (a, c)) in enumerate(todo):
                    ins = pe.matmul(dst, lhs(a, k), rhs(c, k), start=first and n == 0,
                                    stop=last and n == len(todo) - 1)
                return ins

            pe.wait_ge(consts_loaded, 16)
            for stage, b, k, place, step in steps(pe):
                if stage in SHARED:
                    bank = X[SHARED_ORDER.index(place) % 2]
                    prior = bank_before(place, step)
                    if prior is not None:
                        s, pb_, idx = prior
                        if s in ("q", "k"):
                            pe.wait_ge(rest_done, pb_.times(2, 1 if s == "q" else 2))
                        elif s == "wo":
                            pe.wait_ge(x1_done, pb_.times(TT, TT))
                        else:
                            pe.wait_ge(drained[s], pb_.times(PER.get(s, 1), idx + 1))
                if stage in ("xT", "oT", "x2T"):
                    src, done, n = {"xT": (xn, xn_done, TT), "oT": (o_sb, o_done, 16), "x2T": (xn2, xn2_done, TT)}[stage]
                    pe.wait_ge(done, b.times(n, n))
                    for kt in range(KT):
                        for t in range(TT):
                            last = pe.transpose(bank[:, S * kt + P * t:S * kt + P * (t + 1)],
                                                src[:, t, P * kt:P * (kt + 1)], ident_f)
                    last.then_inc(ready[stage], 1)
                if stage in ("q", "k"):
                    n = 0 if stage == "q" else 1
                    if b.trip is None and b.base == 0:
                        pe.wait_ge(lo_split, N_QKV)
                    pe.wait_ge(drained["xT"], b.times(1, 1))
                    for t in range(KT):
                        cols = slice(H * n + P * t, H * n + P * (t + 1))
                        last = three_products(bank[:, S * t:S * (t + 1)], lambda a, kt: (wqkv_h, wqkv_l)[a][:, kt, cols],
                                              lambda a, kt: (xt_h, xt_l)[a][:, kt, :], range(KT), True, True)
                    last.then_inc(ready[stage], 1)
                if stage == "v":
                    for t in range(TT):
                        last = three_products(bank[:, H * t:H * (t + 1)],
                                              lambda a, kt: (xt_h, xt_l)[a][:, kt, P * t:P * (t + 1)],
                                              lambda a, kt: (wqkv_h, wqkv_l)[a][:, kt, 2 * H:3 * H], range(KT), True, True)
                    last.then_inc(ready["v"], 1)
                if stage == "A":
                    q, key = QS[b.parity], KS[b.parity]
                    if k == 0:
                        if b.trip is None and b.base == 0:
                            pe.wait_ge(consts_cast, 4)
                        pe.wait_ge(stack_loaded[b.parity], b.pairs(16 * 12, 16 * 12))
                    for h in (2 * k, 2 * k + 1):
                        if h >= 2 or not (b.trip is None and b.base == 0):
                            pe.wait_ge(a_max, b.times(NH, h - 1))
                        bank = SA[h % 2]
                        pe.matmul(bank[:, 0:S], q[0:DOT_ROWS, h, P:S], key[0:DOT_ROWS, h, :], start=True, stop=False)
                        pe.matmul(bank[:, P:S], ident_b[:, :], mask_a[:, :], start=False, stop=True)
                        pe.matmul(bank[:, S:SC], q[0:DOT_ROWS, h, 0:P], key[0:DOT_ROWS, h, 0:P], start=True, stop=False)
                        pe.matmul(bank[:, S:SC], ident_b[:, :], mask_a[:, :], start=False, stop=True)\
                            .then_inc(a_ready, 1)
                if stage == "mT":
                    pe.wait_ge(m_low, b.times(1, 1))
                    bb = bank[:, :].bitcast(BF16)
                    for p in range(NPART):
                        for t, c in ((0, NBLK), (1, 0)):
                            last = pe.transpose(bb[:, S * p + P * t:S * p + P * (t + 1)],
                                                mpart[:, p, NH * c:NH * (c + NBLK)], ident_b[:, :])
                    last.then_inc(ready["mT"], 1)
                if stage == "B":
                    q, key = QS[b.parity], KS[b.parity]
                    if k == 0:
                        pe.wait_ge(m_loaded, b.times(16, 16))
                        if b.trip is None and b.base == 0:
                            pe.wait_ge(ind_set, 2)
                    for h in (2 * k, 2 * k + 1):
                        if h >= 2 or not (b.trip is None and b.base == 0):
                            pe.wait_ge(exp_done, b.times(NH, h - 1))
                        bank = SB[h % 2]
                        pe.matmul(bank[:, 0:S], key[:, h, 0:P], q[:, h, :], start=True, stop=False)
                        pe.matmul(bank[:, 0:P], ident_b[:, :], mask_b[:, :], start=False, stop=True)
                        pe.matmul(bank[:, S:SC], key[:, h, P:S], q[:, h, P:S], start=True, stop=False)
                        pe.matmul(bank[:, S:SC], ident_b[:, :], mask_b[:, :], start=False, stop=True)\
                            .then_inc(b_ready, 1)
                if stage == "PV":
                    if k == 0:
                        pe.wait_ge(drained["v"], b.times(1, 1))
                    pe.wait_ge(exp_done, b.times(NH, 2 * k + 2))
                    if k >= 2 or not (b.trip is None and b.base == 0):
                        pe.wait_ge(pv_drained, b.times(8, k - 1))
                    for n in range(2):
                        v = VB[b.parity]
                        o = PO[k % 2][:, NC_ * VW * n:NC_ * VW * (n + 1)]
                        for dst, src, t in ((0, P, 0), (PW, S, 1), (2 * PW, 0, 0)):
                            last = pe.matmul(o[:, dst:dst + PW], PT[k % 2][:, n, src:src + P], v[:, t, 2 * k + n, :],
                                             start=True, stop=True)
                    last.then_inc(pv_ready, 1)
                if stage == "wo":
                    if b.trip is None and b.base == 0:
                        pe.wait_ge(lo_split, N_WO)
                    pe.wait_ge(drained["oT"], b.times(1, 1))
                    for t in range(TT):
                        last = three_products(bank[:, H * t:H * (t + 1)],
                                              lambda a, kt: (ot_h, ot_l)[a][:, kt, P * t:P * (t + 1)],
                                              lambda a, kt: (wo_h, wo_l)[a][:, kt, :], range(KT), True, True)
                    last.then_inc(ready["wo"], 1)
                if stage == "rt":
                    if b.trip is None and b.base == 0:
                        pe.wait_ge(wr_loaded, 16)
                    pe.wait_ge(drained["x2T"], b.times(1, 1))
                    for t in range(TT):
                        for n in range(2 * KT):
                            src = (x2_h, x2_l)[n % 2][:, n // 2, P * t:P * (t + 1)].bitcast(F32)
                            last = pe.matmul(bank[:, NE * t:NE * (t + 1)], src, wr_sb[:, n // 2, :],
                                             start=(n == 0), stop=(n == 2 * KT - 1))
                    last.then_inc(ready["rt"], 1)
                if stage == "sT":
                    pe.wait_ge(s_low, b.times(1, 1))
                    bb = bank[:, :].bitcast(BF16)
                    for t in range(TT):
                        last = pe.transpose(bb[0:MAX_ROWS, P * t:P * (t + 1)],
                                            spart[:, t, :, :].rearrange("p a e -> p (a e)"), ident_b[:, :])
                    last.then_inc(ready["sT"], 1)
                if stage == "sb":
                    pe.wait_ge(drained["sT"], b.times(1, 1))
                    for n in range(2):
                        last = pe.matmul(bank[:, S * n:S * (n + 1)], sel[:, 2 * k + n, :], st_sb[:, :],
                                         start=True, stop=True)
                    last.then_inc(ready["sb"], 1)
                if stage == "gu":
                    if b.trip is None and b.base == 0 and k == 0:
                        pe.wait_ge(lo_split, N_GU)
                    for g in range(2):
                        last = three_products(bank[:, S * g:S * (g + 1)],
                                              lambda a, kt: (wgu_h, wgu_l)[a][:, k, kt, g, :],
                                              lambda a, kt: (x2_h, x2_l)[a][:, kt, :], range(KT), True, True)
                    last.then_inc(ready["gu"], 1)
                if stage == "dn":
                    if b.trip is None and b.base == 0:
                        pe.wait_ge(lo_split, N_DN)
                    pe.wait_ge(hid_lo, b.times(NE, NE))
                    last = three_products(bank[:, 0:H], lambda a, e: (hid_h, hid_l)[a][:, e, P * k:P * (k + 1)],
                                          lambda a, e: (wdn_h, wdn_l)[a][:, e, :], range(NE), True, True)
                    last.then_inc(ready["dn"], 1)


def constants():
    import numpy as np

    c = np.zeros((P, 728), np.float32)
    p = np.arange(P)
    c[:, 0:P] = np.eye(P)
    blk = p // BS
    own = np.concatenate([np.repeat((BPT + blk)[:, None], NBLK, 1), np.repeat(blk[:, None], BPT, 1)], 1)
    j = np.concatenate([np.arange(NBLK), np.arange(BPT)])[None, :]
    c[:, P:P + NC_] = j > own
    for t in range(TT):
        c[:, P + NC_ + t] = 1.0 / (BPT * t + blk + 1 + 1e-6)
    e = np.arange(NE)
    c[:, 152:216] = (e[None, :] < e[:, None]).reshape(-1)[None, :]
    q, k = p[:, None], p[None, :]
    c[:, 216:344] = np.where((q // BS == k // BS) & (k > q), MASKED, 0.0)
    c[:, 344:472] = np.where(q > k, MASKED, 0.0)
    r = np.arange(MAX_ROWS)
    c[DOT_ROWS:STACK, 472:728] = (np.arange(S)[None, :] // BS) == (r[:, None] % NBLK)
    s = np.zeros((MAX_ROWS, NE, P), np.float32)
    for n in r:
        s[n, n % NE, :] = 1.0
    return c, s.reshape(MAX_ROWS, NE * P)


def kernel(L0_attn_hidden_states, L0_attn_Wq, L0_attn_Wk, L0_attn_Wv, L0_attn_Wo, L0_ffn_router_gate,
           L0_ffn_expert_gate_up, L0_ffn_expert_down):
    import numpy as np
    import concourse.bacc as bacc
    from concourse.bass_utils import run_bass_kernel_spmd

    def on_partitions(w):
        return w.T.reshape(KT, P, -1).transpose(1, 0, 2)

    wqkv = np.concatenate([on_partitions(np.asarray(w)) for w in (L0_attn_Wq, L0_attn_Wk, L0_attn_Wv)], 2)
    wgu = np.asarray(L0_ffn_expert_gate_up).reshape(NE, KT, P, NI, 2).transpose(2, 0, 1, 4, 3)
    c, s = constants()
    arrays = {
        "x": np.asarray(L0_attn_hidden_states), "wqkv": wqkv, "wo": on_partitions(np.asarray(L0_attn_Wo)),
        "wr": on_partitions(np.asarray(L0_ffn_router_gate)), "wgu": wgu,
        "wdn": np.asarray(L0_ffn_expert_down).transpose(1, 0, 2), "consts": c, "selc": s,
    }
    arrays = {n: np.ascontiguousarray(a) for n, a in arrays.items()}
    nc = bacc.Bacc("TRN2", target_bir_lowering=False, num_devices=1)
    args = {n: nc.dram_tensor(n, a.shape, F32, kind="ExternalInput").ap() for n, a in arrays.items()}
    args["out"] = nc.dram_tensor("out", (NB, S, H), F32, kind="ExternalOutput").ap()
    args["parts_d"] = nc.dram_tensor("parts_d", (2, NPART, 2, H, S), BF16, kind="Internal").ap()
    args["max_d"] = nc.dram_tensor("max_d", (NPART, NBLK, NH, S), BF16, kind="Internal").ap()
    preln_block_attention_moe(nc, **args)
    r = run_bass_kernel_spmd(nc, [arrays], core_ids=[0])
    return r.results[0]["out"]
```

```python
from contextlib import ExitStack

import concourse.bass as bass
from concourse import mybir

ALU = mybir.AluOpType
ACT = mybir.ActivationFunctionType
AX = mybir.AxisListType
F32 = mybir.dt.float32
F32R = mybir.dt.float32r
BF16 = mybir.dt.bfloat16

P = 128
NB = 8
S = 256
TT = S // P
H = 256
KT = H // P
NH = 16
HD = H // NH
BS = 32
NBLK = S // BS
BPT = P // BS
NE = 8
NI = 128
EPS = 1e-5
SCALE = 0.25
MASKED = -1.0e30

Q_PART = [0, 1, 2, 0, 1, 0]
K_PART = [0, 0, 0, 1, 1, 2]
NPART = 3
DOT_ROWS = len(Q_PART) * HD
MAX_ROWS = NBLK * NPART
STACK = DOT_ROWS + MAX_ROWS
NC_ = BPT + NBLK
SC = NC_ * BS
VW = HD + 1
PW = BPT * VW
TRIPS = 2

SP_ORDER = (
    "xload1 w0.0-2 qP0 xload2 w0.3 kP0 w0.4 stack0 qP1 w0.5 xload3 kP1 w0.6 stack1 w0.7 mS0 w0.8-9 "
    "xres0 mS1 w0.10 qP2 kP2 stack2 w0.11 qP3 w0.12 xres1",
    "kP3 stack3 mS2 xload4 dx0.0-1 xres2 qP4",
    "kP7 stack7 mS6 xres6 dx4.0 mS7 dx4.1 xres7 dx5.0-1 dx6.0-1 dx7.0-1",
)
ACT_ORDER = (
    "xS0 w0.0-1 qS0 w0.2 kS0 w0.3 xS1 w0.4 vS0 qS1 kS1 xS2 w0.5-8 vS1 qS2 mS0 w0.9 ex0.0 kS2 ex0.1-3 "
    "w0.10 ex0.4 mS1 ex0.5 w0.11 ex0.6-7 xS3 ex1.0 w0.12 vS2 oS0 ex1.1 qS3 kS3 x2S0 ex1.2-3 top0 ex1.4 "
    "sS0 bS0.0 ex1.5 w0.13-14 th0.0 ex1.6 bS0.1 th0.1 hs0.0 th0.2-3 bS0.2 ex1.7 hs0.1 mS2 th0.4 hs0.2 "
    "bS0.3 hs0.3 th0.5 hs0.4 vS3 th0.6 ex2.0 hs0.5 th0.7 hs0.6 ex2.1 hs0.7 oS1",
    "ex2.2 xS4 ex2.3 qS4 x2S1 ex2.4 kS4 top1 sS1 bS1.0 th1.0 ex2.5 th1.1 ex2.6 bS1.1 th1.2-3 hs1.0-1 "
    "bS1.2-3 mS3 ex2.7 th1.4-5 hs1.2-4 vS4 th1.6 ex3.0 hs1.5 th1.7 oS2 hs1.6 ex3.1 hs1.7",
    "ex6.2-4 x2S5 top5 ex6.5-6 sS5 ex6.7 bS5.0 th5.0 mS7 bS5.1 th5.1-2 hs5.0 th5.3 ex7.0 hs5.1 oS6 "
    "bS5.2 ex7.1 hs5.2 bS5.3 th5.4 hs5.3 ex7.2 th5.5 ex7.3 th5.6 hs5.4-6 th5.7 x2S6 ex7.4 hs5.7 ex7.5 "
    "top6 sS6 bS6.0 ex7.6 th6.0-1 bS6.1 hs6.0 ex7.7 th6.2 hs6.1 th6.3 bS6.2-3 th6.4 oS7 hs6.2-4 th6.5-6 "
    "hs6.5 th6.7 x2S7 hs6.6-7 top7 sS7 bS7.0-2 th7.0-1 hs7.0 th7.2-3 hs7.1-2 th7.4-5 hs7.3 bS7.3 "
    "hs7.4-5 th7.6-7 hs7.6-7",
)
POOL_ORDER = (
    "ln0 ln1 qP0 kP0 ln2 qP1 kP1 ms0 ln3 qP2 ms1 kP2 res0 qP3 top0 kP3 hp0.0 ms2 hp0.1 hl0.0-1 hp0.2-3 "
    "hl0.2 hp0.4 hl0.3-4 hp0.5-6 hl0.5 hp0.7 hl0.6-7",
    "ln4 res1 qP4 top1 kP4 hp1.0-1 ms3 hl1.0-1 hp1.2-3 hl1.2 hp1.4 hl1.3-4 hp1.5 hl1.5 hp1.6-7 hl1.6-7",
    "res5 top5 ms7 hp5.0-1 hl5.0-1 hp5.2 res6 hp5.3 hl5.2-3 hp5.4-5 hl5.4 hp5.6 hl5.5-6 hp5.7 hl5.7 "
    "top6 hp6.0 hl6.0 hp6.1-2 hl6.1-2 hp6.3-4 hl6.3-4 res7 hp6.5 hl6.5 hp6.6-7 hl6.6-7 top7 hp7.0 hl7.0 "
    "hp7.1-2 hl7.1 hp7.3 hl7.2 hp7.4 hl7.3 hp7.5 hl7.4-5 hp7.6-7 hl7.6-7",
)
DVE_ORDER = (
    "ln0 nx0 ln1 xS0 w0.0-1 qS0 nx1 w0.2 kS0 w0.3 xS1 w0.4 ln2 nx2 qS1 kS1 w0.5 xS2 w0.6 am0.0-7 w0.7-8 "
    "qS2 ln3 am1.0-7 kS2 w0.9 o0.0 nx3 o0.1-3 w0.10 o0.4-6 xS3 o0.7 w0.11-12 oS0 o1.0 qS3 res0 am2.0 "
    "nm0 kS3 am2.1 x2S0 o1.1 am2.2 top0 am2.3 o1.2 am2.4 o1.3 am2.5 gd0.0 am2.6-7 o1.4 gd0.1-3 o1.5 "
    "gd0.4 w0.13 o1.6 gd0.5 o1.7 am3.0 gd0.6 w0.14",
    "gd0.7 am3.1 ln4 am3.2 nx4 oS1 am3.3 xS4 res1 o2.0 qS4 dx0.0 nm1 o2.1 x2S1 am3.4 kS4 top1 o2.2 "
    "dx0.1 am3.5 o2.3 gd1.0 am3.6 gd1.1 am3.7 o2.4 gd1.2-3 o2.5-6 gd1.4-5 o2.7 gd1.6 am4.0",
    "gd4.7 am7.1 oS5 o6.0 am7.2 res5 am7.3 nm5 o6.1 x2S5 o6.2 am7.4 top5 am7.5 o6.3 am7.6 dx4.0 am7.7 "
    "gd5.0 o6.4 dx4.1 o6.5-6 gd5.1 o6.7 gd5.2-3 oS6 o7.0 res6 gd5.4 o7.1 gd5.5 nm6 gd5.6 o7.2 gd5.7 "
    "x2S6 top6 o7.3 dx5.0 o7.4-5 gd6.0-1 o7.6 dx5.1 gd6.2-3 o7.7 gd6.4 oS7 res7 gd6.5 nm7 gd6.6-7 x2S7 "
    "top7 dx6.0-1 gd7.0-7 dx7.0-1",
)
PE_ORDER = (
    "xT0 q0 k0 xT1 v0 q1 k1 xT2 v1 q2 A0.0-7 k2 A1.0 mT0 A1.1-6 B0.0 A1.7 B0.1 PV0.0 B0.2 PV0.1 B0.3 "
    "PV0.2 B0.4 mT1 PV0.3 B0.5 PV0.4 xT3 B0.6 PV0.5-6 B0.7 v2 B1.0 PV0.7 PV1.0 B1.1 oT0 q3 wo0 k3 A2.0 "
    "PV1.1 A2.1 x2T0 B1.2 A2.2 B1.3 rt0 PV1.2 A2.3 B1.4 PV1.3 B1.5 A2.4 sT0 gu0.0 sb0.0 PV1.4 A2.5 "
    "PV1.5 A2.6 B1.6 sb0.1 A2.7 gu0.1 B1.7 gu0.2-3 sb0.2 PV1.6 mT2 gu0.4 sb0.3 PV1.7 gu0.5 v3 A3.0 "
    "gu0.6",
    "B2.0 gu0.7 B2.1 oT1 A3.1 PV2.0 B2.2 A3.2 PV2.1 A3.3 xT4 B2.3 wo1 q4 dn0.0 B2.4 PV2.2 x2T1 A3.4 k4 "
    "B2.5 rt1 A3.5 PV2.3 dn0.1 sT1 PV2.4 sb1.0 gu1.0-1 A3.6 B2.6 sb1.1 A3.7 B2.7 gu1.2-3 PV2.5 sb1.2-3 "
    "PV2.6 mT3 gu1.4-5 PV2.7 v4 A4.0 gu1.6",
    "B6.0 gu4.7 oT5 A7.1 B6.1 PV6.0 B6.2 A7.2 wo5 PV6.1 A7.3 B6.3 PV6.2 B6.4 A7.4 x2T5 B6.5 PV6.3 rt5 "
    "PV6.4 A7.5 dn4.0 A7.6 sT5 B6.6 PV6.5 A7.7 B6.7 sb5.0 gu5.0 dn4.1 mT7 PV6.6 sb5.1 gu5.1 PV6.7 "
    "gu5.2-3 B7.0 oT6 B7.1 sb5.2 PV7.0 sb5.3 B7.2 wo6 gu5.4 PV7.1 gu5.5-6 B7.3 PV7.2 gu5.7 x2T6 B7.4 "
    "PV7.3 B7.5 rt6 PV7.4 B7.6 dn5.0 sT6 PV7.5 sb6.0 gu6.0-1 B7.7 PV7.6 sb6.1 dn5.1 gu6.2-3 PV7.7 "
    "sb6.2-3 gu6.4 oT7 wo7 gu6.5-7 x2T7 rt7 dn6.0-1 sT7 sb7.0-2 gu7.0-5 sb7.3 gu7.6-7 dn7.0-1",
)

SHARED = ("oT", "dn", "wo", "xT", "q", "k", "x2T", "rt", "sT", "sb", "gu", "mT", "v")
PER = {"A": 8, "B": 8, "PV": 8, "dn": 2, "gu": 8, "sb": 4}


class Seq:

    def __init__(self, trip, base):
        self.trip, self.base = trip, base

    def times(self, n, plus=0):
        fixed = n * self.base + plus
        return fixed if self.trip is None else self.trip * (2 * n) + fixed

    def pairs(self, n, plus=0):
        fixed = n * (self.base // 2) + plus
        return fixed if self.trip is None else self.trip * n + fixed

    @property
    def parity(self):
        return self.base % 2

    def minus(self, n):
        return Seq(self.trip, self.base - n)


def wait(eng, sem, value):
    if isinstance(value, int) and value <= 0:
        return
    eng.wait_ge(sem, value)


def units(text):
    for word in text.split():
        name, _, index = word.partition(".")
        first, _, last = (index or "0").partition("-")
        for k in range(int(first), int(last or first) + 1):
            yield name[:-1], int(name[-1]), k


def walk(eng, order):
    fill, steady, drain = order
    for stage, b, k in units(fill):
        yield stage, Seq(None, b), k
    with eng.Fori(0, TRIPS) as trip:
        for step in range(2):
            for stage, b, k in units(steady):
                yield stage, Seq(trip, b + step), k
    for stage, b, k in units(drain):
        yield stage, Seq(None, b), k


def shared_banks():
    fill, steady, drain = PE_ORDER
    order = list(units(fill))
    start = len([u for u in order if u[0] in SHARED])
    for step in range(2 * TRIPS):
        order += [(stage, b + step, k) for stage, b, k in units(steady)]
    order = [u for u in order + list(units(drain)) if u[0] in SHARED]
    bank = {u: n % 2 for n, u in enumerate(order)}
    before = {u: order[n - 2] for n, u in enumerate(order) if n >= 2}
    n = 2 * len([u for u in units(steady) if u[0] in SHARED])
    assert n % 2 == 0
    for u, v in zip(order[start:start + n], order[start + n:start + 2 * n]):
        (s, b, k), (s2, b2, k2) = before[u], before[v]
        assert (s, b + 2, k) == (s2, b2, k2), "the loop's first products follow others in later trips"
    return bank, before


BANK, BEFORE = shared_banks()


def preln_block_attention_moe(nc, x, wqkv, wo, wr, wgu, wdn, consts, selc, out, parts_d, max_d):
    with ExitStack() as ctx:

        def sb(name, shape, dt):
            return ctx.enter_context(nc.sbuf_tensor(name, shape, dt))

        def pb(name):
            return ctx.enter_context(nc.psum_tensor(name, [P, 512], F32))

        def sem(name):
            return ctx.enter_context(nc.semaphore(name))

        wqkv_h, wqkv_l = (sb(f"wqkv_{n}", [P, KT, 3 * H], F32R) for n in "hl")
        wo_h, wo_l = (sb(f"wo_{n}", [P, KT, H], F32R) for n in "hl")
        wgu_h, wgu_l = (sb(f"wgu_{n}", [P, NE, KT, 2, NI], F32R) for n in "hl")
        wdn_h, wdn_l = (sb(f"wdn_{n}", [P, NE, H], F32R) for n in "hl")
        wr_sb = sb("wr_sb", [P, KT, NE], F32)
        raw = [sb(f"raw{n}", [P, 3 * H], F32) for n in range(2)]
        cst = sb("cst", [P, 216], F32)
        ident_f = cst[:, 0:P]
        excluded = cst[:, P:P + NC_]
        norm = cst[:, P + NC_:P + NC_ + TT]
        before = cst[:, 152:216].rearrange("p (a b) -> p a b", a=NE)
        ident_b = sb("ident_b", [P, P], BF16)
        mask_a = sb("mask_a", [P, P], BF16)
        mask_b = sb("mask_b", [P, P], BF16)
        sel = sb("sel", [MAX_ROWS, NE, P], BF16)
        minus_half = sb("minus_half", [P, TT], F32)
        x_sb = sb("x_sb", [P, TT, H], F32)
        stats = [sb(f"stats{n}", [P, TT, 6], F32) for n in range(2)]
        mv = [sb(f"mv{n}", [P, TT, 2], F32) for n in range(2)]
        veps = [sb(f"veps{n}", [P, TT], F32) for n in range(2)]
        rstd = [sb(f"rstd{n}", [P, TT], F32) for n in range(2)]
        xn = sb("xn", [P, TT, H], F32)
        xt_h, xt_l = (sb(f"xt_{n}", [P, KT, S], F32R) for n in "hl")
        parts = sb("parts", [P, NPART, 2, KT, S], BF16)
        rest = [sb(f"rest{n}", [P, KT, S], F32) for n in range(2)]
        QS = [sb(f"QS{n}", [STACK, NH, S], BF16) for n in range(2)]
        KS = [sb(f"KS{n}", [STACK, NH, S], BF16) for n in range(2)]
        VB = [sb(f"VB{n}", [P, TT, NH, PW], F32) for n in range(2)]
        nmax = sb("nmax", [P, 16, NH], F32)
        mpart = sb("mpart", [P, NPART, 16 * NH], BF16)
        mrest = sb("mrest", [P, 16 * NH], F32)
        mt_sb = sb("mt_sb", [P, NPART, S], BF16)
        PT = [sb(f"PT{n}", [P, 2, SC], F32) for n in range(2)]
        lsum = sb("lsum", [P, 2, NC_], F32)
        linv = sb("linv", [P, 2, NC_], F32)
        oblk = sb("oblk", [P, 2, NC_, HD], F32)
        o_sb = sb("o_sb", [P, TT, H], F32)
        ot_h, ot_l = (sb(f"ot_{n}", [P, KT, S], F32R) for n in "hl")
        xres = sb("xres", [P, TT, H], F32)
        x1 = [sb(f"x1{n}", [P, TT, H], F32) for n in range(2)]
        xn2 = sb("xn2", [P, TT, H], F32)
        x2_h, x2_l = (sb(f"x2_{n}", [P, KT, S], F32R) for n in "hl")
        logit = sb("logit", [P, TT, NE], F32)
        lmax = sb("lmax", [P, TT], F32)
        ldiff = sb("ldiff", [P, TT, NE], F32)
        lexp = sb("lexp", [P, TT, NE], F32)
        above = sb("above", [P, TT, NE, NE], F32)
        equal = sb("equal", [P, TT, NE, NE], F32)
        tied = sb("tied", [P, TT, NE, NE], F32)
        beats = sb("beats", [P, TT, NE, NE], F32)
        rank = sb("rank", [P, TT, NE], F32)
        picked = sb("picked", [P, TT, NE], F32)
        psumm = sb("psumm", [P, TT], F32)
        pinv = sb("pinv", [P, TT], F32)
        score = sb("score", [P, TT, NE], F32)
        spart = sb("spart", [P, TT, NPART, NE], BF16)
        srest = sb("srest", [P, TT, NE], F32)
        st_sb = sb("st_sb", [MAX_ROWS, S], BF16)
        sbc = sb("sbc", [P, NE, S], F32)
        th = [sb(f"th{n}", [P, S], F32) for n in range(2)]
        gsil = [sb(f"gsil{n}", [P, S], F32) for n in range(2)]
        ups = [sb(f"ups{n}", [P, S], F32) for n in range(2)]
        hid = [sb(f"hid{n}", [P, S], F32) for n in range(2)]
        hid_h, hid_l = (sb(f"hid_{n}", [P, NE, S], F32R) for n in "hl")

        SA = [pb(f"SA{n}") for n in range(2)]
        SB = [pb(f"SB{n}") for n in range(2)]
        PO = [pb(f"PO{n}") for n in range(2)]
        X = [pb(f"X{n}") for n in range(2)]

        ready = {s: sem(f"{s}_ready") for s in SHARED}
        drained = {s: sem(f"{s}_drained") for s in SHARED}
        consts_loaded, sel_loaded, raw_loaded = sem("consts_loaded"), sem("sel_loaded"), [sem(f"raw_loaded{n}") for n in range(2)]
        hi_split, lo_split = sem("hi_split"), sem("lo_split")
        wr_loaded = sem("wr_loaded")
        consts_cast = sem("consts_cast")
        half_set = sem("half_set")
        waits_met = sem("waits_met")
        v_cleared = sem("v_cleared")
        ind_set = sem("ind_set")
        x_loaded, xres_loaded = sem("x_loaded"), sem("xres_loaded")
        stats_done = [sem(f"stats_done{n}") for n in range(2)]
        mv_done = [sem(f"mv_done{n}") for n in range(2)]
        veps_done = [sem(f"veps_done{n}") for n in range(2)]
        rstd_done = [sem(f"rstd_done{n}") for n in range(2)]
        xn_done, xn2_done, x1_done = sem("xn_done"), sem("xn2_done"), sem("x1_done")
        hi_copied = {s: sem(f"{s}_hi") for s in ("xT", "oT", "x2T", "q", "k")}
        rest_done, mid_done, low_done = sem("rest_done"), sem("mid_done"), sem("low_done")
        parts_stored = sem("parts_stored")
        stack_loaded = [sem(f"stack_loaded{n}") for n in range(2)]
        a_ready, a_max = sem("a_ready"), sem("a_max")
        m_high, m_rest, m_mid, m_low = sem("m_high"), sem("m_rest"), sem("m_mid"), sem("m_low")
        m_stored, m_loaded = sem("m_stored"), sem("m_loaded")
        b_ready, exp_done = sem("b_ready"), sem("exp_done")
        pv_ready, pv_drained = sem("pv_ready"), sem("pv_drained")
        sum_done, inv_done, o_done = sem("sum_done"), sem("inv_done"), sem("o_done")
        lmax_done, ldiff_done, lexp_done = sem("lmax_done"), sem("ldiff_done"), sem("lexp_done")
        cmp_done, tied_done, beats_done, rank_done = sem("cmp_done"), sem("tied_done"), sem("beats_done"), sem("rank_done")
        picked_done, psumm_done, pinv_done, score_done = sem("picked_done"), sem("psumm_done"), sem("pinv_done"), sem("score_done")
        s_high, s_rest, s_mid, s_low = sem("s_high"), sem("s_rest"), sem("s_mid"), sem("s_low")
        tanh_done, act_done, hid_done, hid_hi, hid_lo = sem("tanh_done"), sem("act_done"), sem("hid_done"), sem("hid_hi"), sem("hid_lo")
        out_stored = [sem(f"out_stored{n}") for n in range(2)]

        chunks = []
        for kt in range(KT):
            chunks.append((wqkv[:, kt, :], 3 * H, wqkv_h[:, kt, :], wqkv_l[:, kt, :]))
        N_QKV = len(chunks)
        chunks.append((wo.rearrange("p k n -> p (k n)"), KT * H,
                       wo_h[:, :, :].rearrange("p k n -> p (k n)"), wo_l[:, :, :].rearrange("p k n -> p (k n)")))
        N_WO = len(chunks)
        for e in range(NE):
            v = [w[:, e:e + 1].rearrange("p e k g n -> p (e k g n)") for w in (wgu, wgu_h[:, :, :, :, :], wgu_l[:, :, :, :, :])]
            chunks.append((v[0], KT * 2 * NI, v[1], v[2]))
        N_GU = len(chunks)
        for e in range(0, NE, 2):
            v = [w[:, e:e + 2].rearrange("p e n -> p (e n)") for w in (wdn, wdn_h[:, :, :], wdn_l[:, :, :])]
            chunks.append((v[0], 2 * H, v[1], v[2]))
        N_DN = len(chunks)

        x_v = x.rearrange("b (t p) h -> b p t h", p=P)
        out_v = out.rearrange("b (t p) h -> b t p h", p=P)

        block = ctx.enter_context(nc.Block())

        def stand_alone(eng):
            eng.sem_inc(waits_met, 1)

        def row(t, b):
            return t[bass.ds(b.times(1), 1)].rearrange("a p t h -> (a p) t h") if b.trip is not None else t[b.base]

        def x_bank(product, b, k=0):
            return X[BANK[product, b.base, k]]

        @block.sync
        def _(sp):
            def load_chunk(n):
                if n >= 2:
                    sp.wait_ge(lo_split, n - 1)
                sp.dma_start(raw[n % 2][:, 0:chunks[n][1]], chunks[n][0]).then_inc(raw_loaded[n % 2], 16)

            sp.dma_start(x_sb[:, :, :], x_v[0]).then_inc(x_loaded, 16)
            sp.sem_inc(out_stored[1], 1)
            sp.dma_start(cst[:, :], consts[:, 0:216]).then_inc(consts_loaded, 16)
            load_chunk(0)
            load_chunk(1)
            sp.dma_start(sbc[:, 0:2, :].rearrange("p a b -> p (a b)"), consts[:, 216:728]).then_inc(sel_loaded, 16)
            sp.dma_start(sbc[0:MAX_ROWS, 2:6, :].rearrange("p a b -> p (a b)"), selc).then_inc(sel_loaded, 16)
            sp.dma_start(wr_sb[:, :, :], wr).then_inc(wr_loaded, 16)

            for stage, b, k in walk(sp, SP_ORDER):
                if stage == "w":
                    load_chunk(k + 2)
                if stage == "xload":
                    wait(sp, xn_done, b.times(TT))
                    stand_alone(sp)
                    sp.dma_start(x_sb[:, :, :], row(x_v, b)).then_inc(x_loaded, 16)
                if stage == "xres":
                    wait(sp, x1_done, b.times(TT))
                    stand_alone(sp)
                    sp.dma_start(xres[:, :, :], row(x_v, b)).then_inc(xres_loaded, 16)
                if stage in ("qP", "kP"):
                    n = 0 if stage == "qP" else 1
                    sp.wait_ge(low_done, b.times(2, n + 1))
                    stand_alone(sp)
                    if n == 0 and not (b.trip is None and b.base < 2):
                        wait(sp, stack_loaded[b.parity], b.pairs(16 * 12))
                        stand_alone(sp)
                    for p in range(NPART):
                        sp.dma_start(parts_d[b.parity, p, n].rearrange("(t q) s -> q t s", q=P),
                                     parts[:, p, n, :, :]).then_inc(parts_stored, 16)
                if stage == "stack":
                    sp.wait_ge(parts_stored, b.times(16 * 6, 16 * 6))
                    stand_alone(sp)
                    if not (b.trip is None and b.base < 2):
                        sp.wait_ge(b_ready, b.times(NH, -NH))
                        stand_alone(sp)
                    for r in range(len(Q_PART)):
                        for n, stk, part in ((0, QS, Q_PART[r]), (1, KS, K_PART[r])):
                            src = parts_d[b.parity, part, n].rearrange("(h d) s -> d h s", d=HD)
                            sp.dma_start(stk[b.parity][HD * r:HD * (r + 1), :, :], src)\
                                .then_inc(stack_loaded[b.parity], 16)
                if stage == "mS":
                    sp.wait_ge(drained["mT"], b.times(1, 1))
                    stand_alone(sp)
                    for p in range(NPART):
                        sp.dma_start(max_d[p].rearrange("j h s -> (j h) s"), mt_sb[:, p, :])\
                            .then_inc(m_stored, 16)
                    sp.wait_ge(m_stored, b.times(16 * NPART, 16 * NPART))
                    stand_alone(sp)
                    sp.dma_start(QS[b.parity][DOT_ROWS:STACK, :, :], max_d.rearrange("p j h s -> (p j) h s"))\
                        .then_inc(m_loaded, 16)
                if stage == "dx":
                    sp.wait_ge(drained["dn"], b.times(TT, k + 1))
                    stand_alone(sp)
                    dst = out_v[bass.ds(b.times(1), 1), k].rearrange("a p h -> (a p) h") if b.trip is not None \
                        else out_v[b.base, k]
                    sp.dma_start(dst, x1[b.parity][:, k, :]).then_inc(out_stored[b.parity], 16)
            for n in range(2):
                sp.wait_ge(out_stored[n], 16 * TT * NB // 2 + n)
                stand_alone(sp)

        @block.scalar
        def _(act):
            def split_hi(n):
                act.wait_ge(raw_loaded[n % 2], 16 * (n // 2 + 1))
                nc.scalar.copy(chunks[n][2], raw[n % 2][:, 0:chunks[n][1]]).then_inc(hi_split, 1)

            act.wait_ge(sel_loaded, 32)
            nc.scalar.copy(mask_a[:, :], sbc[:, 0, 0:P]).then_inc(consts_cast, 1)
            nc.scalar.copy(mask_b[:, :], sbc[:, 0, P:2 * P]).then_inc(consts_cast, 1)
            nc.scalar.copy(sel[:, :, :], sbc[0:MAX_ROWS, 2:6, :].rearrange("p a b -> p (a b)")
                           .rearrange("p (e n) -> p e n", e=NE)).then_inc(consts_cast, 1)
            act.wait_ge(consts_loaded, 16)
            nc.scalar.copy(ident_b[:, :], ident_f).then_inc(consts_cast, 1)
            for n in range(2):
                ind = sbc[DOT_ROWS:STACK, 1, :].unsqueeze(1).to_broadcast([MAX_ROWS, NH, S])
                nc.scalar.copy(KS[n][DOT_ROWS:STACK, :, :], ind).then_inc(ind_set, 1)

            for stage, b, k in walk(act, ACT_ORDER):
                if stage == "w":
                    split_hi(k)
                if stage in ("xS", "oS", "x2S"):
                    product = {"xS": "xT", "oS": "oT", "x2S": "x2T"}[stage]
                    bank = x_bank(product, b)
                    hi = {"xT": xt_h, "oT": ot_h, "x2T": x2_h}[product]
                    reader, n = {"xT": ("v", 1), "oT": ("wo", 1), "x2T": ("gu", NE)}[product]
                    act.wait_ge(ready[product], b.times(1, 1))
                    wait(act, ready[reader], b.times(n))
                    nc.scalar.copy(hi[:, :, :], bank[:, :].rearrange("p (k s) -> p k s", k=KT))\
                        .then_inc(hi_copied[product], 1)
                if stage in ("qS", "kS"):
                    product, n = ("q", 0) if stage == "qS" else ("k", 1)
                    bank = x_bank(product, b)
                    act.wait_ge(ready[product], b.times(1, 1))
                    wait(act, parts_stored, b.times(16 * 6))
                    nc.scalar.copy(parts[:, 0, n, :, :], bank[:, :].rearrange("p (k s) -> p k s", k=KT))\
                        .then_inc(hi_copied[product], 1)
                if stage == "vS":
                    bank = x_bank("v", b)
                    act.wait_ge(ready["v"], b.times(1, 1))
                    if b.trip is None and b.base < 2:
                        act.wait_ge(v_cleared, (BPT + 1) * (b.base + 1))
                    else:
                        act.wait_ge(pv_ready, b.times(8, -8))
                    for j in range(BPT):
                        q = slice(BS * j, BS * (j + 1))
                        dst = VB[b.parity][q, :, :, VW * j:VW * j + HD]
                        src = bank[q, :].rearrange("p (t h d) -> p t h d", t=TT, h=NH)
                        last = nc.scalar.copy(dst, src)
                    last.then_inc(drained["v"], 1)
                if stage == "mS":
                    bank = x_bank("mT", b)[:, :].bitcast(BF16)
                    act.wait_ge(ready["mT"], b.times(1, 1))
                    wait(act, m_stored, b.times(16 * NPART))
                    nc.scalar.copy(mt_sb[:, :, :], bank[:, 0:NPART * S].rearrange("p (a s) -> p a s", a=NPART))\
                        .then_inc(drained["mT"], 1)
                if stage == "ex":
                    if k >= 2 or not (b.trip is None and b.base == 0):
                        act.wait_ge(pv_ready, b.times(8, k - 1))
                    for h in (2 * k, 2 * k + 1):
                        act.wait_ge(b_ready, b.times(NH, h + 1))
                        nc.scalar.activation(PT[k % 2][:, h % 2, :], SB[h % 2][:, 0:SC], ACT.Exp, scale=SCALE)\
                            .then_inc(exp_done, 1)
                if stage == "top":
                    act.wait_ge(ldiff_done, b.times(1, 1))
                    wait(act, picked_done, b.times(1))
                    nc.scalar.activation(lexp[:, :, :], ldiff[:, :, :], ACT.Exp).then_inc(lexp_done, 1)
                if stage == "sS":
                    bank = x_bank("sT", b)[:, :].bitcast(BF16)
                    act.wait_ge(ready["sT"], b.times(1, 1))
                    wait(act, ready["sb"], b.times(4))
                    nc.scalar.copy(st_sb[:, :], bank[0:MAX_ROWS, 0:S]).then_inc(drained["sT"], 1)
                if stage == "bS":
                    bank = x_bank("sb", b, k)
                    act.wait_ge(ready["sb"], b.times(4, k + 1))
                    if not (b.trip is None and b.base == 0):
                        act.wait_ge(drained["gu"], b.times(NE, 2 * k + 2 - NE))
                    nc.scalar.copy(sbc[:, 2 * k:2 * k + 2, :], bank[:, :].rearrange("p (e s) -> p e s", e=2))\
                        .then_inc(drained["sb"], 1)
                if stage == "th":
                    bank = x_bank("gu", b, k)
                    act.wait_ge(ready["gu"], b.times(NE, k + 1))
                    if k >= 2 or not (b.trip is None and b.base == 0):
                        act.wait_ge(drained["gu"], b.times(NE, k - 1))
                    nc.scalar.activation(th[k % 2][:, :], bank[:, 0:S], ACT.Tanh, scale=0.5).then_inc(tanh_done, 1)
                if stage == "hs":
                    act.wait_ge(hid_done, b.times(NE, k + 1))
                    wait(act, ready["dn"], b.times(TT))
                    nc.scalar.copy(hid_h[:, k, :], hid[k % 2][:, :]).then_inc(hid_hi, 1)

        @block.gpsimd
        def _(pool):
            nc.gpsimd.memset(minus_half[:, :], -0.5).then_inc(half_set, 1)
            nc.gpsimd.memset(nmax[:, NC_:16, :], 0.0).then_inc(half_set, 1)
            for n in range(2):
                if n:
                    pool.wait_ge(v_cleared, n * (BPT + 1))
                nc.gpsimd.memset(VB[n][:, :, :, :], 0.0).then_inc(v_cleared, 1)
                for j in range(BPT):
                    pool.wait_ge(v_cleared, n * (BPT + 1) + 1 + j)
                    nc.gpsimd.memset(VB[n][BS * j:BS * (j + 1), :, :, VW * j + HD:VW * (j + 1)], 1.0)\
                        .then_inc(v_cleared, 1)
            pool.wait_ge(half_set, 2)
            pool.wait_ge(v_cleared, 2 * (BPT + 1))

            for stage, b, k in walk(pool, POOL_ORDER):
                if stage in ("ln", "res"):
                    n = 0 if stage == "ln" else 1
                    pool.wait_ge(mv_done[n], b.times(TT, TT))
                    wait(pool, xn2_done if n else xn_done, b.times(TT))
                    stand_alone(pool)
                    nc.gpsimd.tensor_scalar(veps[n][:, :], mv[n][:, :, 1], EPS, None, ALU.add)\
                        .then_inc(veps_done[n], 1)
                    pool.wait_ge(veps_done[n], b.times(1, 1))
                    nc.gpsimd.tensor_tensor(rstd[n][:, :], veps[n][:, :], minus_half[:, :], ALU.pow)\
                        .then_inc(rstd_done[n], 1)
                if stage in ("qP", "kP"):
                    n = 0 if stage == "qP" else 1
                    pool.wait_ge(rest_done, b.times(2, n + 1))
                    wait(pool, parts_stored, b.times(16 * 6))
                    stand_alone(pool)
                    nc.gpsimd.tensor_copy(parts[:, 1, n, :, :], rest[n][:, :, :]).then_inc(mid_done, 1)
                    pool.wait_ge(mid_done, b.times(2, n + 1))
                    nc.gpsimd.tensor_tensor(parts[:, 2, n, :, :], rest[n][:, :, :], parts[:, 1, n, :, :],
                                            ALU.subtract).then_inc(low_done, 1)
                if stage == "ms":
                    m = nmax[:, :, :].rearrange("p c h -> p (c h)")
                    pool.wait_ge(a_max, b.times(NH, NH))
                    wait(pool, ready["mT"], b.times(1))
                    stand_alone(pool)
                    nc.gpsimd.tensor_copy(mpart[:, 0, :], m).then_inc(m_high, 1)
                    pool.wait_ge(m_high, b.times(1, 1))
                    nc.gpsimd.tensor_tensor(mrest[:, :], m, mpart[:, 0, :], ALU.subtract).then_inc(m_rest, 1)
                    pool.wait_ge(m_rest, b.times(1, 1))
                    stand_alone(pool)
                    nc.gpsimd.tensor_copy(mpart[:, 1, :], mrest[:, :]).then_inc(m_mid, 1)
                    pool.wait_ge(m_mid, b.times(1, 1))
                    nc.gpsimd.tensor_tensor(mpart[:, 2, :], mrest[:, :], mpart[:, 1, :], ALU.subtract)\
                        .then_inc(m_low, 1)
                if stage == "top":
                    pool.wait_ge(score_done, b.times(1, 1))
                    wait(pool, ready["sT"], b.times(1))
                    stand_alone(pool)
                    nc.gpsimd.tensor_copy(spart[:, :, 0, :], score[:, :, :]).then_inc(s_high, 1)
                    pool.wait_ge(s_high, b.times(1, 1))
                    nc.gpsimd.tensor_tensor(srest[:, :, :], score[:, :, :], spart[:, :, 0, :], ALU.subtract)\
                        .then_inc(s_rest, 1)
                    pool.wait_ge(s_rest, b.times(1, 1))
                    stand_alone(pool)
                    nc.gpsimd.tensor_copy(spart[:, :, 1, :], srest[:, :, :]).then_inc(s_mid, 1)
                    pool.wait_ge(s_mid, b.times(1, 1))
                    nc.gpsimd.tensor_tensor(spart[:, :, 2, :], srest[:, :, :], spart[:, :, 1, :], ALU.subtract)\
                        .then_inc(s_low, 1)
                if stage == "hp":
                    pool.wait_ge(act_done, b.times(NE, k + 1))
                    pool.wait_ge(drained["gu"], b.times(NE, k + 1))
                    if k >= 2 or not (b.trip is None and b.base == 0):
                        pool.wait_ge(hid_hi, b.times(NE, k - 1))
                        pool.wait_ge(hid_lo, b.times(NE, k - 1))
                    nc.gpsimd.tensor_tensor(hid[k % 2][:, :], gsil[k % 2][:, :], ups[k % 2][:, :], ALU.mult)\
                        .then_inc(hid_done, 1)
                if stage == "hl":
                    pool.wait_ge(hid_hi, b.times(NE, k + 1))
                    pool.wait_ge(hid_done, b.times(NE, k + 1))
                    wait(pool, ready["dn"], b.times(TT))
                    nc.gpsimd.tensor_tensor(hid_l[:, k, :], hid[k % 2][:, :], hid_h[:, k, :].bitcast(F32),
                                            ALU.subtract).then_inc(hid_lo, 1)

        @block.vector
        def _(dve):
            def split_lo(n):
                dve.wait_ge(hi_split, n + 1)
                dve.wait_ge(raw_loaded[n % 2], 16 * (n // 2 + 1))
                nc.vector.tensor_tensor(chunks[n][3], raw[n % 2][:, 0:chunks[n][1]], chunks[n][2].bitcast(F32),
                                        ALU.subtract).then_inc(lo_split, 1)

            def layernorm_stats(n, b, src):
                for t in range(TT):
                    nc.vector.bn_stats(stats[n][:, t, :], src[:, t, :]).then_inc(stats_done[n], 1)
                for t in range(TT):
                    dve.wait_ge(stats_done[n], b.times(TT, t + 1))
                    stand_alone(dve)
                    nc.vector.bn_aggr(mv[n][:, t, :], stats[n][:, t, :]).then_inc(mv_done[n], 1)

            def normalise(n, b, dst, src, done):
                dve.wait_ge(rstd_done[n], b.times(1, 1))
                for t in range(TT):
                    nc.vector.tensor_scalar(dst[:, t, :], src[:, t, :], mv[n][:, t, 0:1], rstd[n][:, t:t + 1],
                                            ALU.subtract, ALU.mult).then_inc(done, 1)

            for stage, b, k in walk(dve, DVE_ORDER):
                if stage == "ln":
                    dve.wait_ge(x_loaded, b.times(16, 16))
                    layernorm_stats(0, b, x_sb)
                if stage == "nx":
                    wait(dve, ready["xT"], b.times(1))
                    normalise(0, b, xn, x_sb, xn_done)
                if stage == "w":
                    split_lo(k)
                if stage in ("xS", "oS", "x2S"):
                    product = {"xS": "xT", "oS": "oT", "x2S": "x2T"}[stage]
                    bank = x_bank(product, b)
                    hi, lo = {"xT": (xt_h, xt_l), "oT": (ot_h, ot_l), "x2T": (x2_h, x2_l)}[product]
                    reader, n = {"xT": ("v", 1), "oT": ("wo", 1), "x2T": ("gu", NE)}[product]
                    dve.wait_ge(hi_copied[product], b.times(1, 1))
                    wait(dve, ready[reader], b.times(n))
                    nc.vector.tensor_tensor(lo[:, :, :], bank[:, :].rearrange("p (k s) -> p k s", k=KT),
                                            hi[:, :, :].bitcast(F32), ALU.subtract).then_inc(drained[product], 1)
                if stage in ("qS", "kS"):
                    product, n = ("q", 0) if stage == "qS" else ("k", 1)
                    bank = x_bank(product, b)
                    dve.wait_ge(hi_copied[product], b.times(1, 1))
                    wait(dve, low_done, b.times(2))
                    nc.vector.tensor_tensor(rest[n][:, :, :], bank[:, :].rearrange("p (k s) -> p k s", k=KT),
                                            parts[:, 0, n, :, :], ALU.subtract)\
                        .then_inc(rest_done, 1)
                if stage == "am":
                    if k == 0:
                        wait(dve, m_low, b.times(1))
                    for h in (2 * k, 2 * k + 1):
                        dve.wait_ge(a_ready, b.times(NH, h + 1))
                        nc.vector.tensor_reduce(nmax[:, 0:NC_, h], SA[h % 2][:, 0:SC]
                                                .rearrange("p (c s) -> p c s", s=BS), AX.X, ALU.max, negate=True)\
                            .then_inc(a_max, 1)
                if stage == "o":
                    po = PO[k % 2][:, 0:2 * NC_ * VW].rearrange("p (h c v) -> p h c v", h=2, v=VW)
                    dve.wait_ge(pv_ready, b.times(8, k + 1))
                    wait(dve, inv_done, b.times(8, k))
                    nc.vector.tensor_tensor(lsum[:, :, :], po[:, :, :, HD],
                                            excluded.unsqueeze(1).to_broadcast([P, 2, NC_]), ALU.add)\
                        .then_inc(sum_done, 1)
                    dve.wait_ge(sum_done, b.times(8, k + 1))
                    wait(dve, pv_drained, b.times(8, k))
                    nc.vector.reciprocal(linv[:, :, :], lsum[:, :, :]).then_inc(inv_done, 1)
                    dve.wait_ge(inv_done, b.times(8, k + 1))
                    wait(dve, o_done, b.times(16, 2 * k))
                    for h in range(2):
                        last = nc.vector.tensor_tensor(oblk[:, h, :, :], po[:, h, :, 0:HD],
                                                linv[:, h, :].unsqueeze(2).to_broadcast([P, NC_, HD]), ALU.mult)
                    last.then_inc(pv_drained, 1)
                    dve.wait_ge(pv_drained, b.times(8, k + 1))
                    if k == 0:
                        wait(dve, ready["oT"], b.times(1))
                    for t, c in ((0, slice(NBLK, NC_)), (1, slice(0, NBLK))):
                        nc.vector.tensor_reduce(
                            o_sb[:, t, 2 * HD * k:2 * HD * (k + 1)].rearrange("p (h d) -> p h d", h=2),
                            oblk[:, :, c, :].rearrange("p h c d -> p h d c"), AX.X, ALU.add).then_inc(o_done, 1)
                if stage == "res":
                    bank = x_bank("wo", b)
                    y = x1[b.parity]
                    dve.wait_ge(ready["wo"], b.times(1, 1))
                    dve.wait_ge(xres_loaded, b.times(16, 16))
                    if not (b.trip is None and b.base < 2):
                        dve.wait_ge(out_stored[b.parity], b.pairs(16 * TT, b.parity))
                    for t in range(TT):
                        nc.vector.scalar_tensor_tensor(out=y[:, t, :], in0=bank[:, H * t:H * (t + 1)],
                                                       scalar=norm[:, t:t + 1], in1=xres[:, t, :],
                                                       op0=ALU.mult, op1=ALU.add).then_inc(x1_done, 1)
                    dve.wait_ge(x1_done, b.times(TT, TT))
                    layernorm_stats(1, b, y)
                if stage == "nm":
                    wait(dve, ready["x2T"], b.times(1))
                    normalise(1, b, xn2, x1[b.parity], xn2_done)
                if stage == "top":
                    bank = x_bank("rt", b)
                    dve.wait_ge(ready["rt"], b.times(1, 1))
                    nc.vector.tensor_copy(logit[:, :, :], bank[:, 0:TT * NE].rearrange("p (t e) -> p t e", t=TT))\
                        .then_inc(drained["rt"], 1)
                    dve.wait_ge(drained["rt"], b.times(1, 1))
                    nc.vector.tensor_reduce(lmax[:, :], logit[:, :, :], AX.X, ALU.max).then_inc(lmax_done, 1)
                    dve.wait_ge(lmax_done, b.times(1, 1))
                    wait(dve, lexp_done, b.times(1))
                    nc.vector.tensor_tensor(ldiff[:, :, :], logit[:, :, :],
                                            lmax[:, :].unsqueeze(2).to_broadcast([P, TT, NE]), ALU.subtract)\
                        .then_inc(ldiff_done, 1)
                    for t in range(TT):
                        mine = logit[:, t, :].unsqueeze(2).to_broadcast([P, NE, NE])
                        other = logit[:, t, :].unsqueeze(1).to_broadcast([P, NE, NE])
                        nc.vector.tensor_tensor(equal[:, t], other, mine, ALU.is_equal).then_inc(cmp_done, 1)
                        nc.vector.tensor_tensor(above[:, t], other, mine, ALU.is_gt).then_inc(cmp_done, 1)
                    dve.wait_ge(cmp_done, b.times(2 * TT, 2 * TT))
                    nc.vector.tensor_tensor(tied[:, :, :, :], equal[:, :, :, :],
                                            before.unsqueeze(1).to_broadcast([P, TT, NE, NE]), ALU.mult)\
                        .then_inc(tied_done, 1)
                    dve.wait_ge(tied_done, b.times(1, 1))
                    nc.vector.tensor_tensor(beats[:, :, :, :], tied[:, :, :, :], above[:, :, :, :], ALU.add)\
                        .then_inc(beats_done, 1)
                    dve.wait_ge(beats_done, b.times(1, 1))
                    nc.vector.tensor_reduce(rank[:, :, :], beats[:, :, :, :], AX.X, ALU.add).then_inc(rank_done, 1)
                    dve.wait_ge(rank_done, b.times(1, 1))
                    dve.wait_ge(lexp_done, b.times(1, 1))
                    nc.vector.scalar_tensor_tensor(out=picked[:, :, :], in0=rank[:, :, :], scalar=1.5,
                                                   in1=lexp[:, :, :], op0=ALU.is_lt, op1=ALU.mult)\
                        .then_inc(picked_done, 1)
                    dve.wait_ge(picked_done, b.times(1, 1))
                    nc.vector.tensor_reduce(psumm[:, :], picked[:, :, :], AX.X, ALU.add).then_inc(psumm_done, 1)
                    dve.wait_ge(psumm_done, b.times(1, 1))
                    wait(dve, s_low, b.times(1))
                    wait(dve, s_rest, b.times(1))
                    nc.vector.reciprocal(pinv[:, :], psumm[:, :]).then_inc(pinv_done, 1)
                    dve.wait_ge(pinv_done, b.times(1, 1))
                    nc.vector.tensor_tensor(score[:, :, :], picked[:, :, :],
                                            pinv[:, :].unsqueeze(2).to_broadcast([P, TT, NE]), ALU.mult)\
                        .then_inc(score_done, 1)
                if stage == "gd":
                    bank = x_bank("gu", b, k)
                    dve.wait_ge(tanh_done, b.times(NE, k + 1))
                    dve.wait_ge(drained["sb"], b.times(4, k // 2 + 1))
                    if k >= 2 or not (b.trip is None and b.base == 0):
                        dve.wait_ge(hid_done, b.times(NE, k - 1))
                    nc.vector.scalar_tensor_tensor(out=gsil[k % 2][:, :], in0=th[k % 2][:, :], scalar=1.0,
                                                   in1=bank[:, 0:S], op0=ALU.add, op1=ALU.mult).then_inc(act_done, 1)
                    last = nc.vector.scalar_tensor_tensor(out=ups[k % 2][:, :], in0=bank[:, S:2 * S], scalar=0.5,
                                                          in1=sbc[:, k, :], op0=ALU.mult, op1=ALU.mult)
                    last.then_inc(drained["gu"], 1)
                if stage == "dx":
                    bank = x_bank("dn", b, k)
                    dve.wait_ge(ready["dn"], b.times(TT, k + 1))
                    dve.wait_ge(x1_done, b.times(TT, TT))
                    nc.vector.tensor_tensor(x1[b.parity][:, k, :], bank[:, 0:H], x1[b.parity][:, k, :], ALU.add)\
                        .then_inc(drained["dn"], 1)

        @block.tensor
        def _(pe):
            def three_products(dst, lhs, rhs, ks, first, last):
                todo = [(k, p) for k in ks for p in ((0, 0), (0, 1), (1, 0))]
                for n, (k, (a, c)) in enumerate(todo):
                    ins = pe.matmul(dst, lhs(a, k), rhs(c, k), start=first and n == 0,
                                    stop=last and n == len(todo) - 1)
                return ins

            pe.wait_ge(consts_loaded, 16)
            for stage, b, k in walk(pe, PE_ORDER):
                if stage in SHARED:
                    bank = x_bank(stage, b, k)
                    if (stage, b.base, k) in BEFORE:
                        s, base, idx = BEFORE[stage, b.base, k]
                        pb_ = Seq(b.trip, base)
                        if s in ("q", "k"):
                            pe.wait_ge(rest_done, pb_.times(2, 1 if s == "q" else 2))
                        elif s == "wo":
                            pe.wait_ge(x1_done, pb_.times(TT, TT))
                        else:
                            pe.wait_ge(drained[s], pb_.times(PER.get(s, 1), idx + 1))
                if stage in ("xT", "oT", "x2T"):
                    src, done, n = {"xT": (xn, xn_done, TT), "oT": (o_sb, o_done, 16), "x2T": (xn2, xn2_done, TT)}[stage]
                    pe.wait_ge(done, b.times(n, n))
                    for kt in range(KT):
                        for t in range(TT):
                            last = pe.transpose(bank[:, S * kt + P * t:S * kt + P * (t + 1)],
                                                src[:, t, P * kt:P * (kt + 1)], ident_f)
                    last.then_inc(ready[stage], 1)
                if stage in ("q", "k"):
                    n = 0 if stage == "q" else 1
                    if b.trip is None and b.base == 0:
                        pe.wait_ge(lo_split, N_QKV)
                    pe.wait_ge(drained["xT"], b.times(1, 1))
                    for t in range(KT):
                        cols = slice(H * n + P * t, H * n + P * (t + 1))
                        last = three_products(bank[:, S * t:S * (t + 1)], lambda a, kt: (wqkv_h, wqkv_l)[a][:, kt, cols],
                                              lambda a, kt: (xt_h, xt_l)[a][:, kt, :], range(KT), True, True)
                    last.then_inc(ready[stage], 1)
                if stage == "v":
                    for t in range(TT):
                        last = three_products(bank[:, H * t:H * (t + 1)],
                                              lambda a, kt: (xt_h, xt_l)[a][:, kt, P * t:P * (t + 1)],
                                              lambda a, kt: (wqkv_h, wqkv_l)[a][:, kt, 2 * H:3 * H], range(KT), True, True)
                    last.then_inc(ready["v"], 1)
                if stage == "A":
                    q, key = QS[b.parity], KS[b.parity]
                    if k == 0:
                        if b.trip is None and b.base == 0:
                            pe.wait_ge(consts_cast, 4)
                        pe.wait_ge(stack_loaded[b.parity], b.pairs(16 * 12, 16 * 12))
                    for h in (2 * k, 2 * k + 1):
                        if h >= 2 or not (b.trip is None and b.base == 0):
                            pe.wait_ge(a_max, b.times(NH, h - 1))
                        bank = SA[h % 2]
                        pe.matmul(bank[:, 0:S], q[0:DOT_ROWS, h, P:S], key[0:DOT_ROWS, h, :], start=True, stop=False)
                        pe.matmul(bank[:, P:S], ident_b[:, :], mask_a[:, :], start=False, stop=True)
                        pe.matmul(bank[:, S:SC], q[0:DOT_ROWS, h, 0:P], key[0:DOT_ROWS, h, 0:P], start=True, stop=False)
                        pe.matmul(bank[:, S:SC], ident_b[:, :], mask_a[:, :], start=False, stop=True)\
                            .then_inc(a_ready, 1)
                if stage == "mT":
                    pe.wait_ge(m_low, b.times(1, 1))
                    bb = bank[:, :].bitcast(BF16)
                    for p in range(NPART):
                        for t, c in ((0, NBLK), (1, 0)):
                            last = pe.transpose(bb[:, S * p + P * t:S * p + P * (t + 1)],
                                                mpart[:, p, NH * c:NH * (c + NBLK)], ident_b[:, :])
                    last.then_inc(ready["mT"], 1)
                if stage == "B":
                    q, key = QS[b.parity], KS[b.parity]
                    if k == 0:
                        pe.wait_ge(m_loaded, b.times(16, 16))
                        if b.trip is None and b.base == 0:
                            pe.wait_ge(ind_set, 2)
                    for h in (2 * k, 2 * k + 1):
                        if h >= 2 or not (b.trip is None and b.base == 0):
                            pe.wait_ge(exp_done, b.times(NH, h - 1))
                        bank = SB[h % 2]
                        pe.matmul(bank[:, 0:S], key[:, h, 0:P], q[:, h, :], start=True, stop=False)
                        pe.matmul(bank[:, 0:P], ident_b[:, :], mask_b[:, :], start=False, stop=True)
                        pe.matmul(bank[:, S:SC], key[:, h, P:S], q[:, h, P:S], start=True, stop=False)
                        pe.matmul(bank[:, S:SC], ident_b[:, :], mask_b[:, :], start=False, stop=True)\
                            .then_inc(b_ready, 1)
                if stage == "PV":
                    if k == 0:
                        pe.wait_ge(drained["v"], b.times(1, 1))
                    pe.wait_ge(exp_done, b.times(NH, 2 * k + 2))
                    if k >= 2 or not (b.trip is None and b.base == 0):
                        pe.wait_ge(pv_drained, b.times(8, k - 1))
                    for n in range(2):
                        v = VB[b.parity]
                        o = PO[k % 2][:, NC_ * VW * n:NC_ * VW * (n + 1)]
                        for dst, src, t in ((0, P, 0), (PW, S, 1), (2 * PW, 0, 0)):
                            last = pe.matmul(o[:, dst:dst + PW], PT[k % 2][:, n, src:src + P], v[:, t, 2 * k + n, :],
                                             start=True, stop=True)
                    last.then_inc(pv_ready, 1)
                if stage == "wo":
                    if b.trip is None and b.base == 0:
                        pe.wait_ge(lo_split, N_WO)
                    pe.wait_ge(drained["oT"], b.times(1, 1))
                    for t in range(TT):
                        last = three_products(bank[:, H * t:H * (t + 1)],
                                              lambda a, kt: (ot_h, ot_l)[a][:, kt, P * t:P * (t + 1)],
                                              lambda a, kt: (wo_h, wo_l)[a][:, kt, :], range(KT), True, True)
                    last.then_inc(ready["wo"], 1)
                if stage == "rt":
                    if b.trip is None and b.base == 0:
                        pe.wait_ge(wr_loaded, 16)
                    pe.wait_ge(drained["x2T"], b.times(1, 1))
                    for t in range(TT):
                        for n in range(2 * KT):
                            src = (x2_h, x2_l)[n % 2][:, n // 2, P * t:P * (t + 1)].bitcast(F32)
                            last = pe.matmul(bank[:, NE * t:NE * (t + 1)], src, wr_sb[:, n // 2, :],
                                             start=(n == 0), stop=(n == 2 * KT - 1))
                    last.then_inc(ready["rt"], 1)
                if stage == "sT":
                    pe.wait_ge(s_low, b.times(1, 1))
                    bb = bank[:, :].bitcast(BF16)
                    for t in range(TT):
                        last = pe.transpose(bb[0:MAX_ROWS, P * t:P * (t + 1)],
                                            spart[:, t, :, :].rearrange("p a e -> p (a e)"), ident_b[:, :])
                    last.then_inc(ready["sT"], 1)
                if stage == "sb":
                    pe.wait_ge(drained["sT"], b.times(1, 1))
                    for n in range(2):
                        last = pe.matmul(bank[:, S * n:S * (n + 1)], sel[:, 2 * k + n, :], st_sb[:, :],
                                         start=True, stop=True)
                    last.then_inc(ready["sb"], 1)
                if stage == "gu":
                    if b.trip is None and b.base == 0 and k == 0:
                        pe.wait_ge(lo_split, N_GU)
                    for g in range(2):
                        last = three_products(bank[:, S * g:S * (g + 1)],
                                              lambda a, kt: (wgu_h, wgu_l)[a][:, k, kt, g, :],
                                              lambda a, kt: (x2_h, x2_l)[a][:, kt, :], range(KT), True, True)
                    last.then_inc(ready["gu"], 1)
                if stage == "dn":
                    if b.trip is None and b.base == 0:
                        pe.wait_ge(lo_split, N_DN)
                    pe.wait_ge(hid_lo, b.times(NE, NE))
                    last = three_products(bank[:, 0:H], lambda a, e: (hid_h, hid_l)[a][:, e, P * k:P * (k + 1)],
                                          lambda a, e: (wdn_h, wdn_l)[a][:, e, :], range(NE), True, True)
                    last.then_inc(ready["dn"], 1)


def constants():
    import numpy as np

    c = np.zeros((P, 728), np.float32)
    p = np.arange(P)
    c[:, 0:P] = np.eye(P)
    blk = p // BS
    own = np.concatenate([np.repeat((BPT + blk)[:, None], NBLK, 1), np.repeat(blk[:, None], BPT, 1)], 1)
    j = np.concatenate([np.arange(NBLK), np.arange(BPT)])[None, :]
    c[:, P:P + NC_] = j > own
    for t in range(TT):
        c[:, P + NC_ + t] = 1.0 / (BPT * t + blk + 1 + 1e-6)
    e = np.arange(NE)
    c[:, 152:216] = (e[None, :] < e[:, None]).reshape(-1)[None, :]
    q, k = p[:, None], p[None, :]
    c[:, 216:344] = np.where((q // BS == k // BS) & (k > q), MASKED, 0.0)
    c[:, 344:472] = np.where(q > k, MASKED, 0.0)
    r = np.arange(MAX_ROWS)
    c[DOT_ROWS:STACK, 472:728] = (np.arange(S)[None, :] // BS) == (r[:, None] % NBLK)
    s = np.zeros((MAX_ROWS, NE, P), np.float32)
    for n in r:
        s[n, n % NE, :] = 1.0
    return c, s.reshape(MAX_ROWS, NE * P)


def kernel(L0_attn_hidden_states, L0_attn_Wq, L0_attn_Wk, L0_attn_Wv, L0_attn_Wo, L0_ffn_router_gate,
           L0_ffn_expert_gate_up, L0_ffn_expert_down):
    import numpy as np
    import concourse.bacc as bacc
    from concourse.bass_utils import run_bass_kernel_spmd

    def on_partitions(w):
        return w.T.reshape(KT, P, -1).transpose(1, 0, 2)

    wqkv = np.concatenate([on_partitions(np.asarray(w)) for w in (L0_attn_Wq, L0_attn_Wk, L0_attn_Wv)], 2)
    wgu = np.asarray(L0_ffn_expert_gate_up).reshape(NE, KT, P, NI, 2).transpose(2, 0, 1, 4, 3)
    c, s = constants()
    arrays = {
        "x": np.asarray(L0_attn_hidden_states), "wqkv": wqkv, "wo": on_partitions(np.asarray(L0_attn_Wo)),
        "wr": on_partitions(np.asarray(L0_ffn_router_gate)), "wgu": wgu,
        "wdn": np.asarray(L0_ffn_expert_down).transpose(1, 0, 2), "consts": c, "selc": s,
    }
    arrays = {n: np.ascontiguousarray(a) for n, a in arrays.items()}
    nc = bacc.Bacc("TRN2", target_bir_lowering=False, num_devices=1)
    args = {n: nc.dram_tensor(n, a.shape, F32, kind="ExternalInput").ap() for n, a in arrays.items()}
    args["out"] = nc.dram_tensor("out", (NB, S, H), F32, kind="ExternalOutput").ap()
    args["parts_d"] = nc.dram_tensor("parts_d", (2, NPART, 2, H, S), BF16, kind="Internal").ap()
    args["max_d"] = nc.dram_tensor("max_d", (NPART, NBLK, NH, S), BF16, kind="Internal").ap()
    preln_block_attention_moe(nc, **args)
    r = run_bass_kernel_spmd(nc, [arrays], core_ids=[0])
    return r.results[0]["out"]
```

```python
from contextlib import ExitStack

import concourse.bass as bass
from concourse import mybir

ALU = mybir.AluOpType
ACT = mybir.ActivationFunctionType
AX = mybir.AxisListType
F32 = mybir.dt.float32
F32R = mybir.dt.float32r
BF16 = mybir.dt.bfloat16

P = 128
NB = 8
S = 256
TT = S // P
H = 256
KT = H // P
NH = 16
HD = H // NH
BS = 32
NBLK = S // BS
BPT = P // BS
NE = 8
NI = 128
EPS = 1e-5
SCALE = 0.25
MASKED = -1.0e30

Q_PART = [0, 1, 2, 0, 1, 0]
K_PART = [0, 0, 0, 1, 1, 2]
NPART = 3
DOT_ROWS = len(Q_PART) * HD
MAX_ROWS = NBLK * NPART
STACK = DOT_ROWS + MAX_ROWS
NC_ = BPT + NBLK
SC = NC_ * BS
VW = HD + 1
PW = BPT * VW
CONSTS = 224
TRIPS = 2

SP_ORDER = (
    "xload1 w0.0-1 xres0 xload2 qP0 kP0 w0.2 stack0 xload3 qP1 w0.3 kP1 w0.4 stack1 mS0 w0.5 qP2 kP2 "
    "w0.6-8 mS1 stack2 w0.9-10 qP3 w0.11 kP3 w0.12 xres1 stack3",
    "xload4 mS2 qP4 kP4 dx0.0-1 xres2 stack4",
    "mS6 dx4.0 xres6 dx4.1 mS7 dx5.0 xres7 dx5.1 dx6.0-1 dx7.0-1",
)
ACT_ORDER = (
    "w0.0-1 xS0 qS0 w0.2 kS0 w0.3 vS0 xS1 vS1 qS1 xS2 w0.4 kS1 qS2 w0.5-6 kS2 mS0 ex0.0 w0.7 ex0.1-2 "
    "w0.8 ex0.3 mS1 ex0.4-5 w0.9-10 ex0.6-7 ex1.0 vS2 oS0 ex1.1-2 xS3 ex1.3 x2S0 qS3 ex1.4 lS0 kS3 top0 "
    "w0.11 sS0 w0.12 bS0.0 ex1.5 bS0.1-2 ex1.6 th0.0-2 w0.13 ex1.7 w0.14 th0.3 hs0.0-1 bS0.3 mS2 hs0.2 "
    "th0.4 hs0.3-4 th0.5 vS3 th0.6 ex2.0 hs0.5 oS1 hs0.6 ex2.1 th0.7 hs0.7 ex2.2-3",
    "x2S1 xS4 lS1 ex2.4-5 qS4 top1 kS4 sS1 ex2.6 bS1.0 th1.0-1 bS1.1 th1.2 hs1.0 bS1.2 ex2.7 bS1.3 "
    "th1.3 mS3 hs1.1-2 th1.4 hs1.3 th1.5 hs1.4 vS4 hs1.5 th1.6 ex3.0-1 oS2 hs1.6 th1.7 hs1.7 ex3.2-3",
    "x2S5 lS5 top5 ex6.4-5 sS5 bS5.0 ex6.6 th5.0 bS5.1 mS7 bS5.2 hs5.0 ex6.7 th5.1-2 ex7.0 th5.3 oS6 "
    "hs5.1 bS5.3 ex7.1 hs5.2-3 th5.4-6 ex7.2 th5.7 x2S6 lS6 ex7.3 hs5.4 top6 hs5.5 ex7.4-5 sS6 ex7.6 "
    "hs5.6 bS6.0 th6.0 hs5.7 bS6.1 ex7.7 bS6.2 th6.1-2 bS6.3 th6.3 hs6.0 oS7 hs6.1-2 th6.4 hs6.3 "
    "th6.5-6 hs6.4-5 th6.7 x2S7 hs6.6-7 lS7 top7 sS7 bS7.0-1 th7.0-1 hs7.0 th7.2 hs7.1 th7.3 bS7.2 "
    "hs7.2 bS7.3 th7.4 hs7.3 th7.5 hs7.4-5 th7.6-7 hs7.6-7",
)
POOL_ORDER = (
    "ln0 z0 ln1 qP0 kP0 ln2 qP1 kP1 ms0 qP2 ln3 kP2 ms1 res0 qP3 top0 kP3 hp0.0-1 ms2 hl0.0-1 hp0.2-3 "
    "hl0.2-3 hp0.4 hl0.4 hp0.5-6 hl0.5 hp0.7 hl0.6-7 res1",
    "ln4 top1 qP4 kP4 hp1.0 ms3 hp1.1 hl1.0 hp1.2 hl1.1 hp1.3 hl1.2 hp1.4 hl1.3 hp1.5 hl1.4 hp1.6 hl1.5 "
    "hp1.7 hl1.6-7 res2",
    "top5 ms7 hp5.0-1 hl5.0-1 hp5.2-3 res6 hl5.2 hp5.4 hl5.3 hp5.5 hl5.4 hp5.6 top6 hl5.5-6 hp5.7 hl5.7 "
    "hp6.0-1 hl6.0 hp6.2 hl6.1-2 hp6.3-4 hl6.3 res7 hp6.5 hl6.4-5 hp6.6-7 hl6.6-7 top7 hp7.0-1 hl7.0-1 "
    "hp7.2-3 hl7.2-3 hp7.4-5 hl7.4-5 hp7.6-7 hl7.6-7",
)
DVE_ORDER = (
    "ln0 nx0 w0.0-1 xS0 ln1 qS0 kS0 nx1 xS1 w0.2-3 ln2 qS1 nx2 xS2 w0.4 kS1 am0.0-7 w0.5 ln3 w0.6 qS2 "
    "kS2 am1.0-6 w0.7 am1.7 nx3 o0.0 w0.8 o0.1-7 w0.9-10 oS0 o1.0 res0 o1.1 nm0 xS3 o1.2 x2S0 am2.0 qS3 "
    "am2.1 top0 am2.2 kS3 am2.3 o1.3 am2.4 w0.11 am2.5 gd0.0 w0.12 am2.6 gd0.1 am2.7 gd0.2 o1.4 gd0.3 "
    "o1.5-6 gd0.4 w0.13 am3.0 gd0.5 o1.7 am3.1 w0.14 gd0.6 am3.2 oS1 o2.0 gd0.7",
    "am3.3 res1 ln4 am3.4 nm1 nx4 dx0.0 x2S1 o2.1 xS4 o2.2 top1 qS4 dx0.1 o2.3 kS4 am3.5 o2.4 am3.6 "
    "gd1.0 am3.7 gd1.1 o2.5 gd1.2 o2.6 gd1.3 o2.7 gd1.4 am4.0 gd1.5 am4.1 gd1.6 am4.2 oS2 o3.0 gd1.7",
    "am7.3 res5 o6.1 nm5 am7.4 dx4.0 x2S5 am7.5 o6.2 top5 am7.6 dx4.1 am7.7 o6.3-4 gd5.0 o6.5-6 gd5.1-2 "
    "o6.7 gd5.3 oS6 o7.0 res6 gd5.4-5 nm6 gd5.6 o7.1 gd5.7 x2S6 o7.2 top6 o7.3-4 gd6.0-1 o7.5 dx5.0 "
    "gd6.2 o7.6-7 gd6.3 dx5.1 oS7 gd6.4 res7 gd6.5 nm7 gd6.6-7 x2S7 top7 dx6.0-1 gd7.0-7 dx7.0-1",
)
PE_ORDER = (
    "xT0 q0 k0 v0 xT1 v1 q1 k1 xT2 q2 A0.0-7 k2 A1.0 mT0 A1.1-6 B0.0 A1.7 B0.1 PV0.0 B0.2 PV0.1 B0.3 "
    "PV0.2 mT1 B0.4 PV0.3 B0.5 PV0.4 B0.6 PV0.5 B0.7 PV0.6-7 B1.0 v2 PV1.0 oT0 B1.1 xT3 wo0 B1.2 PV1.1 "
    "B1.3 A2.0 PV1.2-3 x2T0 q3 B1.4 rt0 A2.1 lt0 k3 A2.2 B1.5 PV1.4 A2.3 sT0 sb0.0-1 A2.4 sb0.2 B1.6 "
    "gu0.0 A2.5 gu0.1 A2.6 gu0.2 A2.7 B1.7 PV1.5 gu0.3 sb0.3 PV1.6 mT2 gu0.4 PV1.7 gu0.5 A3.0 v3 A3.1 "
    "gu0.6 B2.0",
    "oT1 A3.2 B2.1 PV2.0 gu0.7 A3.3 B2.2 wo1 PV2.1 B2.3 A3.4 dn0.0 x2T1 PV2.2 xT4 B2.4 A3.5 rt1 PV2.3 "
    "lt1 B2.5 q4 dn0.1 k4 sT1 B2.6 PV2.4 sb1.0 gu1.0 A3.6 gu1.1 A3.7 B2.7 sb1.1 PV2.5 gu1.2 sb1.2 PV2.6 "
    "sb1.3 gu1.3 mT3 PV2.7 gu1.4-5 A4.0 v4 A4.1 gu1.6 B3.0",
    "oT5 A7.2 B6.1 PV6.0 gu4.7 A7.3 wo5 B6.2 PV6.1 A7.4 B6.3 dn4.0 x2T5 PV6.2 A7.5 rt5 B6.4 A7.6 lt5 "
    "dn4.1 B6.5 PV6.3 A7.7 sT5 PV6.4 sb5.0 B6.6 gu5.0 PV6.5 sb5.1 B6.7 mT7 sb5.2 PV6.6 gu5.1-2 PV6.7 "
    "gu5.3 B7.0 oT6 B7.1 PV7.0 sb5.3 wo6 gu5.4 B7.2 gu5.5-6 PV7.1 gu5.7 x2T6 PV7.2 rt6 B7.3 lt6 B7.4 "
    "PV7.3 B7.5 PV7.4 B7.6 sT6 PV7.5 sb6.0 B7.7 gu6.0 sb6.1 PV7.6 sb6.2 gu6.1 dn5.0 gu6.2 sb6.3 PV7.7 "
    "gu6.3 dn5.1 oT7 gu6.4 wo7 gu6.5-7 x2T7 rt7 lt7 dn6.0-1 sT7 sb7.0-1 gu7.0-3 sb7.2-3 gu7.4-7 dn7.0-1",
)

SHARED = ("oT", "dn", "wo", "xT", "q", "k", "x2T", "rt", "lt", "sT", "sb", "gu", "mT", "v")
PER = {"A": 8, "B": 8, "PV": 8, "dn": 2, "gu": 8, "sb": 4}


class Seq:

    def __init__(self, trip, base):
        self.trip, self.base = trip, base

    def times(self, n, plus=0):
        fixed = n * self.base + plus
        return fixed if self.trip is None else self.trip * (2 * n) + fixed

    def pairs(self, n, plus=0):
        fixed = n * (self.base // 2) + plus
        return fixed if self.trip is None else self.trip * n + fixed

    @property
    def parity(self):
        return self.base % 2

    def minus(self, n):
        return Seq(self.trip, self.base - n)


def wait(eng, sem, value):
    if isinstance(value, int) and value <= 0:
        return
    eng.wait_ge(sem, value)


def units(text):
    for word in text.split():
        name, _, index = word.partition(".")
        first, _, last = (index or "0").partition("-")
        for k in range(int(first), int(last or first) + 1):
            yield name[:-1], int(name[-1]), k


def walk(eng, order):
    fill, steady, drain = order
    for stage, b, k in units(fill):
        yield stage, Seq(None, b), k
    with eng.Fori(0, TRIPS) as trip:
        for step in range(2):
            for stage, b, k in units(steady):
                yield stage, Seq(trip, b + step), k
    for stage, b, k in units(drain):
        yield stage, Seq(None, b), k


def shared_banks():
    fill, steady, drain = PE_ORDER
    order = list(units(fill))
    start = len([u for u in order if u[0] in SHARED])
    for step in range(2 * TRIPS):
        order += [(stage, b + step, k) for stage, b, k in units(steady)]
    order = [u for u in order + list(units(drain)) if u[0] in SHARED]
    bank = {u: n % 2 for n, u in enumerate(order)}
    before = {u: order[n - 2] for n, u in enumerate(order) if n >= 2}
    n = 2 * len([u for u in units(steady) if u[0] in SHARED])
    assert n % 2 == 0
    for u, v in zip(order[start:start + n], order[start + n:start + 2 * n]):
        (s, b, k), (s2, b2, k2) = before[u], before[v]
        assert (s, b + 2, k) == (s2, b2, k2), "the loop's first products follow others in later trips"
    return bank, before


BANK, BEFORE = shared_banks()


def preln_block_attention_moe(nc, x, wqkv, wo, wr, wgu, wdn, consts, tables, blocks, selc, out, parts_d, max_d):
    with ExitStack() as ctx:

        def sb(name, shape, dt):
            return ctx.enter_context(nc.sbuf_tensor(name, shape, dt))

        def pb(name):
            return ctx.enter_context(nc.psum_tensor(name, [P, 512], F32))

        def sem(name):
            return ctx.enter_context(nc.semaphore(name))

        wqkv_h, wqkv_l = (sb(f"wqkv_{n}", [P, KT, 3 * H], F32R) for n in "hl")
        wo_h, wo_l = (sb(f"wo_{n}", [P, KT, H], F32R) for n in "hl")
        wgu_h, wgu_l = (sb(f"wgu_{n}", [P, NE, KT, 2, NI], F32R) for n in "hl")
        wdn_h, wdn_l = (sb(f"wdn_{n}", [P, NE, H], F32R) for n in "hl")
        wr_sb = sb("wr_sb", [P, KT, NE], F32)
        wr_parts = sb("wr_parts", [P, KT, 2, NE], F32R)
        raw = [sb(f"raw{n}", [P, 3 * H], F32) for n in range(2)]
        cst = sb("cst", [P, CONSTS], F32)
        ident_f = cst[:, 0:P]
        excluded = cst[:, P:P + NC_]
        norm = cst[:, P + NC_:P + NC_ + TT]
        before = cst[:, 152:216].rearrange("p (a b) -> p a b", a=NE)
        add_parts = cst[0:2 * NE, 216:CONSTS]
        tables_b = sb("tables_b", [P, 3, P], BF16)
        ident_b, mask_a, mask_b = (tables_b[:, n, :] for n in range(3))
        sel = sb("sel", [MAX_ROWS, NE, P], BF16)
        minus_half = sb("minus_half", [P, TT], F32)
        x_sb = sb("x_sb", [P, TT, H], F32)
        stats = [sb(f"stats{n}", [P, TT, 6], F32) for n in range(2)]
        mv = [sb(f"mv{n}", [P, TT, 2], F32) for n in range(2)]
        veps = [sb(f"veps{n}", [P, TT], F32) for n in range(2)]
        rstd = [sb(f"rstd{n}", [P, TT], F32) for n in range(2)]
        xn = sb("xn", [P, TT, H], F32)
        xt_h, xt_l = (sb(f"xt_{n}", [P, KT, S], F32R) for n in "hl")
        parts = sb("parts", [P, 2, KT, NPART, S], BF16)
        rest = [sb(f"rest{n}", [P, KT, S], F32) for n in range(2)]
        QS = [sb(f"QS{n}", [STACK, NH, S], BF16) for n in range(2)]
        KS = [sb(f"KS{n}", [STACK, NH, S], BF16) for n in range(2)]
        VB = [sb(f"VB{n}", [P, TT, NH, PW], F32) for n in range(2)]
        nmax = sb("nmax", [P, 16, NH], F32)
        mpart = sb("mpart", [P, NPART, 16 * NH], BF16)
        mrest = sb("mrest", [P, 16 * NH], F32)
        mt_sb = sb("mt_sb", [P, NPART, S], BF16)
        PT = [sb(f"PT{n}", [P, 2, SC], F32) for n in range(2)]
        lsum = sb("lsum", [P, 2, NC_], F32)
        linv = sb("linv", [P, 2, NC_], F32)
        oblk = sb("oblk", [P, 2, NC_, HD], F32)
        o_sb = sb("o_sb", [P, TT, H], F32)
        ot_h, ot_l = (sb(f"ot_{n}", [P, KT, S], F32R) for n in "hl")
        xres = sb("xres", [P, TT, H], F32)
        x1 = [sb(f"x1{n}", [P, TT, H], F32) for n in range(2)]
        xn2 = sb("xn2", [P, TT, H], F32)
        x2_h, x2_l = (sb(f"x2_{n}", [P, KT, S], F32R) for n in "hl")
        lparts = sb("lparts", [2 * NE, S], F32)
        logit = sb("logit", [P, TT, NE], F32)
        lmax = sb("lmax", [P, TT], F32)
        ldiff = sb("ldiff", [P, TT, NE], F32)
        lexp = sb("lexp", [P, TT, NE], F32)
        above = sb("above", [P, TT, NE, NE], F32)
        equal = sb("equal", [P, TT, NE, NE], F32)
        beats = sb("beats", [P, TT, NE, NE], F32)
        rank = sb("rank", [P, TT, NE], F32)
        picked = sb("picked", [P, TT, NE], F32)
        psumm = sb("psumm", [P, TT], F32)
        pinv = sb("pinv", [P, TT], F32)
        score = sb("score", [P, TT, NE], F32)
        spart = sb("spart", [P, TT, NPART, NE], BF16)
        srest = sb("srest", [P, TT, NE], F32)
        st_sb = sb("st_sb", [MAX_ROWS, S], BF16)
        sbc = sb("sbc", [P, NE, S], F32)
        th = [sb(f"th{n}", [P, S], F32) for n in range(2)]
        gsil = [sb(f"gsil{n}", [P, S], F32) for n in range(2)]
        ups = [sb(f"ups{n}", [P, S], F32) for n in range(2)]
        hid = [sb(f"hid{n}", [P, S], F32) for n in range(2)]
        hid_h, hid_l = (sb(f"hid_{n}", [P, NE, S], F32R) for n in "hl")

        SA = [pb(f"SA{n}") for n in range(2)]
        SB = [pb(f"SB{n}") for n in range(2)]
        PO = [pb(f"PO{n}") for n in range(2)]
        X = [pb(f"X{n}") for n in range(2)]

        ready = {s: sem(f"{s}_ready") for s in SHARED}
        drained = {s: sem(f"{s}_drained") for s in SHARED}
        consts_loaded, sel_loaded, raw_loaded = sem("consts_loaded"), sem("sel_loaded"), [sem(f"raw_loaded{n}") for n in range(2)]
        hi_split, lo_split = sem("hi_split"), sem("lo_split")
        wr_loaded, wr_split = sem("wr_loaded"), sem("wr_split")
        tables_loaded, blocks_loaded = sem("tables_loaded"), sem("blocks_loaded")
        half_set = sem("half_set")
        waits_met = sem("waits_met")
        v_cleared = sem("v_cleared")
        x_loaded, xres_loaded = sem("x_loaded"), sem("xres_loaded")
        stats_done = [sem(f"stats_done{n}") for n in range(2)]
        mv_done = [sem(f"mv_done{n}") for n in range(2)]
        veps_done = [sem(f"veps_done{n}") for n in range(2)]
        rstd_done = [sem(f"rstd_done{n}") for n in range(2)]
        xn_done, xn2_done, x1_done = sem("xn_done"), sem("xn2_done"), sem("x1_done")
        hi_copied = {s: sem(f"{s}_hi") for s in ("xT", "oT", "x2T", "q", "k")}
        rest_done, mid_done, low_done = sem("rest_done"), sem("mid_done"), sem("low_done")
        parts_stored = sem("parts_stored")
        stack_loaded = [sem(f"stack_loaded{n}") for n in range(2)]
        a_ready, a_max = sem("a_ready"), sem("a_max")
        m_high, m_rest, m_mid, m_low = sem("m_high"), sem("m_rest"), sem("m_mid"), sem("m_low")
        m_stored, m_loaded = sem("m_stored"), sem("m_loaded")
        b_ready, exp_done = sem("b_ready"), sem("exp_done")
        pv_ready, pv_drained = sem("pv_ready"), sem("pv_drained")
        sum_done, inv_done, o_done = sem("sum_done"), sem("inv_done"), sem("o_done")
        lmax_done, ldiff_done, lexp_done = sem("lmax_done"), sem("ldiff_done"), sem("lexp_done")
        cmp_done, tied_done, beats_done, rank_done = sem("cmp_done"), sem("tied_done"), sem("beats_done"), sem("rank_done")
        picked_done, psumm_done, pinv_done, score_done = sem("picked_done"), sem("psumm_done"), sem("pinv_done"), sem("score_done")
        s_high, s_rest, s_mid, s_low = sem("s_high"), sem("s_rest"), sem("s_mid"), sem("s_low")
        tanh_done, act_done, hid_done, hid_hi, hid_lo = sem("tanh_done"), sem("act_done"), sem("hid_done"), sem("hid_hi"), sem("hid_lo")
        out_stored = [sem(f"out_stored{n}") for n in range(2)]

        chunks = []
        for kt in range(KT):
            chunks.append((wqkv[:, kt, :], 3 * H, wqkv_h[:, kt, :], wqkv_l[:, kt, :]))
        N_QKV = len(chunks)
        chunks.append((wo.rearrange("p k n -> p (k n)"), KT * H,
                       wo_h[:, :, :].rearrange("p k n -> p (k n)"), wo_l[:, :, :].rearrange("p k n -> p (k n)")))
        N_WO = len(chunks)
        for e in range(NE):
            v = [w[:, e:e + 1].rearrange("p e k g n -> p (e k g n)") for w in (wgu, wgu_h[:, :, :, :, :], wgu_l[:, :, :, :, :])]
            chunks.append((v[0], KT * 2 * NI, v[1], v[2]))
        N_GU = len(chunks)
        for e in range(0, NE, 2):
            v = [w[:, e:e + 2].rearrange("p e n -> p (e n)") for w in (wdn, wdn_h[:, :, :], wdn_l[:, :, :])]
            chunks.append((v[0], 2 * H, v[1], v[2]))
        N_DN = len(chunks)

        x_v = x.rearrange("b (t p) h -> b p t h", p=P)
        out_v = out.rearrange("b (t p) h -> b t p h", p=P)

        block = ctx.enter_context(nc.Block())

        def stand_alone(eng):
            eng.sem_inc(waits_met, 1)

        def row(t, b):
            return t[bass.ds(b.times(1), 1)].rearrange("a p t h -> (a p) t h") if b.trip is not None else t[b.base]

        def x_bank(product, b, k=0):
            return X[BANK[product, b.base, k]]

        @block.sync
        def _(sp):
            def load_chunk(n):
                if n >= 2:
                    sp.wait_ge(lo_split, n - 1)
                sp.dma_start(raw[n % 2][:, 0:chunks[n][1]], chunks[n][0]).then_inc(raw_loaded[n % 2], 16)

            sp.dma_start(x_sb[:, :, :], x_v[0]).then_inc(x_loaded, 16)
            sp.sem_inc(out_stored[1], 1)
            sp.dma_start(cst[:, :], consts).then_inc(consts_loaded, 16)
            load_chunk(0)
            load_chunk(1)
            sp.dma_start(tables_b[:, :, :], tables.bitcast(BF16).rearrange("p (a n) -> p a n", a=3)).then_inc(tables_loaded, 16)
            sp.dma_start(wr_sb[:, :, :], wr).then_inc(wr_loaded, 16)
            for n in range(2):
                ind = blocks.bitcast(BF16).unsqueeze(1).to_broadcast([MAX_ROWS, NH, S])
                sp.dma_start(KS[n][DOT_ROWS:STACK, :, :], ind).then_inc(blocks_loaded, 16)
            sp.dma_start(sel[:, :, :].rearrange("p e n -> p (e n)"), selc.bitcast(BF16)).then_inc(sel_loaded, 16)

            for stage, b, k in walk(sp, SP_ORDER):
                if stage == "w":
                    load_chunk(k + 2)
                if stage == "xload":
                    wait(sp, xn_done, b.times(TT))
                    stand_alone(sp)
                    sp.dma_start(x_sb[:, :, :], row(x_v, b)).then_inc(x_loaded, 16)
                if stage == "xres":
                    wait(sp, x1_done, b.times(TT))
                    stand_alone(sp)
                    sp.dma_start(xres[:, :, :], row(x_v, b)).then_inc(xres_loaded, 16)
                if stage in ("qP", "kP"):
                    n = 0 if stage == "qP" else 1
                    sp.wait_ge(low_done, b.times(2, n + 1))
                    stand_alone(sp)
                    if n == 0 and not (b.trip is None and b.base < 2):
                        wait(sp, stack_loaded[b.parity], b.pairs(16 * 12))
                        stand_alone(sp)
                    sp.dma_start(parts_d[b.parity, n].rearrange("(t q) p s -> q t (p s)", q=P),
                                 parts[:, n, :, :, :].rearrange("q t p s -> q t (p s)")).then_inc(parts_stored, 16)
                if stage == "stack":
                    sp.wait_ge(parts_stored, b.times(16 * 2, 16 * 2))
                    stand_alone(sp)
                    if not (b.trip is None and b.base < 2):
                        sp.wait_ge(b_ready, b.times(NH, -NH))
                        stand_alone(sp)
                    for r in range(len(Q_PART)):
                        for n, stk, part in ((0, QS, Q_PART[r]), (1, KS, K_PART[r])):
                            src = parts_d[b.parity, n, :, part, :].rearrange("(h d) s -> d h s", d=HD)
                            sp.dma_start(stk[b.parity][HD * r:HD * (r + 1), :, :], src)\
                                .then_inc(stack_loaded[b.parity], 16)
                if stage == "mS":
                    sp.wait_ge(drained["mT"], b.times(1, 1))
                    stand_alone(sp)
                    sp.dma_start(max_d.rearrange("p j h s -> (j h) p s"), mt_sb[:, :, :]).then_inc(m_stored, 16)
                    sp.wait_ge(m_stored, b.times(16, 16))
                    stand_alone(sp)
                    sp.dma_start(QS[b.parity][DOT_ROWS:STACK, :, :], max_d.rearrange("p j h s -> (p j) h s"))\
                        .then_inc(m_loaded, 16)
                if stage == "dx":
                    sp.wait_ge(drained["dn"], b.times(TT, k + 1))
                    stand_alone(sp)
                    dst = out_v[bass.ds(b.times(1), 1), k].rearrange("a p h -> (a p) h") if b.trip is not None \
                        else out_v[b.base, k]
                    sp.dma_start(dst, x1[b.parity][:, k, :]).then_inc(out_stored[b.parity], 16)
            for n in range(2):
                sp.wait_ge(out_stored[n], 16 * TT * NB // 2 + n)
                stand_alone(sp)

        @block.scalar
        def _(act):
            def split_hi(n):
                act.wait_ge(raw_loaded[n % 2], 16 * (n // 2 + 1))
                nc.scalar.copy(chunks[n][2], raw[n % 2][:, 0:chunks[n][1]]).then_inc(hi_split, 1)

            for stage, b, k in walk(act, ACT_ORDER):
                if stage == "w":
                    split_hi(k)
                if stage == "w" and k == 1:
                    act.wait_ge(wr_loaded, 16)
                    nc.scalar.copy(wr_parts[:, :, 0, :], wr_sb[:, :, :]).then_inc(wr_split, 1)
                if stage in ("xS", "oS", "x2S"):
                    product = {"xS": "xT", "oS": "oT", "x2S": "x2T"}[stage]
                    bank = x_bank(product, b)
                    hi = {"xT": xt_h, "oT": ot_h, "x2T": x2_h}[product]
                    reader, n = {"xT": ("v", 1), "oT": ("wo", 1), "x2T": ("gu", NE)}[product]
                    act.wait_ge(ready[product], b.times(1, 1))
                    wait(act, ready[reader], b.times(n))
                    nc.scalar.copy(hi[:, :, :], bank[:, :].rearrange("p (k s) -> p k s", k=KT))\
                        .then_inc(hi_copied[product], 1)
                if stage in ("qS", "kS"):
                    product, n = ("q", 0) if stage == "qS" else ("k", 1)
                    bank = x_bank(product, b)
                    act.wait_ge(ready[product], b.times(1, 1))
                    wait(act, parts_stored, b.times(16 * 2))
                    nc.scalar.copy(parts[:, n, :, 0, :], bank[:, :].rearrange("p (k s) -> p k s", k=KT))\
                        .then_inc(hi_copied[product], 1)
                if stage == "vS":
                    bank = x_bank("v", b)
                    act.wait_ge(ready["v"], b.times(1, 1))
                    if b.trip is None and b.base < 2:
                        act.wait_ge(v_cleared, (BPT + 1) * (b.base + 1))
                    else:
                        act.wait_ge(pv_ready, b.times(8, -8))
                    for j in range(BPT):
                        q = slice(BS * j, BS * (j + 1))
                        dst = VB[b.parity][q, :, :, VW * j:VW * j + HD]
                        src = bank[q, :].rearrange("p (t h d) -> p t h d", t=TT, h=NH)
                        last = nc.scalar.copy(dst, src)
                    last.then_inc(drained["v"], 1)
                if stage == "mS":
                    bank = x_bank("mT", b)[:, :].bitcast(BF16)
                    act.wait_ge(ready["mT"], b.times(1, 1))
                    wait(act, m_stored, b.times(16))
                    nc.scalar.copy(mt_sb[:, :, :], bank[:, 0:NPART * S].rearrange("p (a s) -> p a s", a=NPART))\
                        .then_inc(drained["mT"], 1)
                if stage == "ex":
                    if k >= 2 or not (b.trip is None and b.base == 0):
                        act.wait_ge(pv_ready, b.times(8, k - 1))
                    for h in (2 * k, 2 * k + 1):
                        act.wait_ge(b_ready, b.times(NH, h + 1))
                        nc.scalar.activation(PT[k % 2][:, h % 2, :], SB[h % 2][:, 0:SC], ACT.Exp, scale=SCALE)\
                            .then_inc(exp_done, 1)
                if stage == "lS":
                    bank = x_bank("rt", b)
                    act.wait_ge(ready["rt"], b.times(1, 1))
                    wait(act, ready["lt"], b.times(1))
                    nc.scalar.copy(lparts[:, :], bank[0:2 * NE, 0:S]).then_inc(drained["rt"], 1)
                if stage == "top":
                    act.wait_ge(ldiff_done, b.times(1, 1))
                    wait(act, picked_done, b.times(1))
                    nc.scalar.activation(lexp[:, :, :], ldiff[:, :, :], ACT.Exp).then_inc(lexp_done, 1)
                if stage == "sS":
                    bank = x_bank("sT", b)[:, :].bitcast(BF16)
                    act.wait_ge(ready["sT"], b.times(1, 1))
                    wait(act, ready["sb"], b.times(4))
                    nc.scalar.copy(st_sb[:, :], bank[0:MAX_ROWS, 0:S]).then_inc(drained["sT"], 1)
                if stage == "bS":
                    bank = x_bank("sb", b, k)
                    act.wait_ge(ready["sb"], b.times(4, k + 1))
                    if not (b.trip is None and b.base == 0):
                        act.wait_ge(drained["gu"], b.times(NE, 2 * k + 2 - NE))
                    nc.scalar.copy(sbc[:, 2 * k:2 * k + 2, :], bank[:, :].rearrange("p (e s) -> p e s", e=2))\
                        .then_inc(drained["sb"], 1)
                if stage == "th":
                    bank = x_bank("gu", b, k)
                    act.wait_ge(ready["gu"], b.times(NE, k + 1))
                    if k >= 2 or not (b.trip is None and b.base == 0):
                        act.wait_ge(drained["gu"], b.times(NE, k - 1))
                    nc.scalar.activation(th[k % 2][:, :], bank[:, 0:S], ACT.Tanh, scale=0.5).then_inc(tanh_done, 1)
                if stage == "hs":
                    act.wait_ge(hid_done, b.times(NE, k + 1))
                    wait(act, ready["dn"], b.times(TT))
                    nc.scalar.copy(hid_h[:, k, :], hid[k % 2][:, :]).then_inc(hid_hi, 1)

        @block.gpsimd
        def _(pool):
            nc.gpsimd.memset(minus_half[:, :], -0.5).then_inc(half_set, 1)
            nc.gpsimd.memset(nmax[:, NC_:16, :], 0.0).then_inc(half_set, 1)
            pool.wait_ge(half_set, 2)

            for stage, b, k in walk(pool, POOL_ORDER):
                if stage == "z":
                    for n in range(2):
                        if n:
                            pool.wait_ge(v_cleared, n * (BPT + 1))
                        nc.gpsimd.memset(VB[n][:, :, :, :], 0.0).then_inc(v_cleared, 1)
                        for j in range(BPT):
                            pool.wait_ge(v_cleared, n * (BPT + 1) + 1 + j)
                            nc.gpsimd.memset(VB[n][BS * j:BS * (j + 1), :, :, VW * j + HD:VW * (j + 1)], 1.0)\
                                .then_inc(v_cleared, 1)
                    pool.wait_ge(v_cleared, 2 * (BPT + 1))
                if stage in ("ln", "res"):
                    n = 0 if stage == "ln" else 1
                    pool.wait_ge(mv_done[n], b.times(TT, TT))
                    wait(pool, xn2_done if n else xn_done, b.times(TT))
                    stand_alone(pool)
                    nc.gpsimd.tensor_scalar(veps[n][:, :], mv[n][:, :, 1], EPS, None, ALU.add)\
                        .then_inc(veps_done[n], 1)
                    pool.wait_ge(veps_done[n], b.times(1, 1))
                    nc.gpsimd.tensor_tensor(rstd[n][:, :], veps[n][:, :], minus_half[:, :], ALU.pow)\
                        .then_inc(rstd_done[n], 1)
                if stage in ("qP", "kP"):
                    n = 0 if stage == "qP" else 1
                    pool.wait_ge(rest_done, b.times(2, n + 1))
                    wait(pool, parts_stored, b.times(16 * 2))
                    stand_alone(pool)
                    nc.gpsimd.tensor_copy(parts[:, n, :, 1, :], rest[n][:, :, :]).then_inc(mid_done, 1)
                    pool.wait_ge(mid_done, b.times(2, n + 1))
                    nc.gpsimd.tensor_tensor(parts[:, n, :, 2, :], rest[n][:, :, :], parts[:, n, :, 1, :],
                                            ALU.subtract).then_inc(low_done, 1)
                if stage == "ms":
                    m = nmax[:, :, :].rearrange("p c h -> p (c h)")
                    pool.wait_ge(a_max, b.times(NH, NH))
                    wait(pool, ready["mT"], b.times(1))
                    stand_alone(pool)
                    nc.gpsimd.tensor_copy(mpart[:, 0, :], m).then_inc(m_high, 1)
                    pool.wait_ge(m_high, b.times(1, 1))
                    nc.gpsimd.tensor_tensor(mrest[:, :], m, mpart[:, 0, :], ALU.subtract).then_inc(m_rest, 1)
                    pool.wait_ge(m_rest, b.times(1, 1))
                    stand_alone(pool)
                    nc.gpsimd.tensor_copy(mpart[:, 1, :], mrest[:, :]).then_inc(m_mid, 1)
                    pool.wait_ge(m_mid, b.times(1, 1))
                    nc.gpsimd.tensor_tensor(mpart[:, 2, :], mrest[:, :], mpart[:, 1, :], ALU.subtract)\
                        .then_inc(m_low, 1)
                if stage == "top":
                    pool.wait_ge(score_done, b.times(1, 1))
                    wait(pool, ready["sT"], b.times(1))
                    stand_alone(pool)
                    nc.gpsimd.tensor_copy(spart[:, :, 0, :], score[:, :, :]).then_inc(s_high, 1)
                    pool.wait_ge(s_high, b.times(1, 1))
                    nc.gpsimd.tensor_tensor(srest[:, :, :], score[:, :, :], spart[:, :, 0, :], ALU.subtract)\
                        .then_inc(s_rest, 1)
                    pool.wait_ge(s_rest, b.times(1, 1))
                    stand_alone(pool)
                    nc.gpsimd.tensor_copy(spart[:, :, 1, :], srest[:, :, :]).then_inc(s_mid, 1)
                    pool.wait_ge(s_mid, b.times(1, 1))
                    nc.gpsimd.tensor_tensor(spart[:, :, 2, :], srest[:, :, :], spart[:, :, 1, :], ALU.subtract)\
                        .then_inc(s_low, 1)
                if stage == "hp":
                    pool.wait_ge(act_done, b.times(NE, k + 1))
                    pool.wait_ge(drained["gu"], b.times(NE, k + 1))
                    if k >= 2 or not (b.trip is None and b.base == 0):
                        pool.wait_ge(hid_hi, b.times(NE, k - 1))
                        pool.wait_ge(hid_lo, b.times(NE, k - 1))
                    nc.gpsimd.tensor_tensor(hid[k % 2][:, :], gsil[k % 2][:, :], ups[k % 2][:, :], ALU.mult)\
                        .then_inc(hid_done, 1)
                if stage == "hl":
                    pool.wait_ge(hid_hi, b.times(NE, k + 1))
                    pool.wait_ge(hid_done, b.times(NE, k + 1))
                    wait(pool, ready["dn"], b.times(TT))
                    nc.gpsimd.tensor_tensor(hid_l[:, k, :], hid[k % 2][:, :], hid_h[:, k, :].bitcast(F32),
                                            ALU.subtract).then_inc(hid_lo, 1)

        @block.vector
        def _(dve):
            def split_lo(n):
                dve.wait_ge(hi_split, n + 1)
                dve.wait_ge(raw_loaded[n % 2], 16 * (n // 2 + 1))
                nc.vector.tensor_tensor(chunks[n][3], raw[n % 2][:, 0:chunks[n][1]], chunks[n][2].bitcast(F32),
                                        ALU.subtract).then_inc(lo_split, 1)

            def layernorm_stats(n, b, src):
                for t in range(TT):
                    nc.vector.bn_stats(stats[n][:, t, :], src[:, t, :]).then_inc(stats_done[n], 1)
                for t in range(TT):
                    dve.wait_ge(stats_done[n], b.times(TT, t + 1))
                    stand_alone(dve)
                    nc.vector.bn_aggr(mv[n][:, t, :], stats[n][:, t, :]).then_inc(mv_done[n], 1)

            def normalise(n, b, dst, src, done):
                dve.wait_ge(rstd_done[n], b.times(1, 1))
                for t in range(TT):
                    nc.vector.tensor_scalar(dst[:, t, :], src[:, t, :], mv[n][:, t, 0:1], rstd[n][:, t:t + 1],
                                            ALU.subtract, ALU.mult).then_inc(done, 1)

            for stage, b, k in walk(dve, DVE_ORDER):
                if stage == "w" and k == 2:
                    dve.wait_ge(wr_split, 1)
                    nc.vector.tensor_tensor(wr_parts[:, :, 1, :], wr_sb[:, :, :], wr_parts[:, :, 0, :].bitcast(F32),
                                            ALU.subtract).then_inc(wr_split, 1)
                if stage == "ln":
                    dve.wait_ge(x_loaded, b.times(16, 16))
                    layernorm_stats(0, b, x_sb)
                if stage == "nx":
                    wait(dve, ready["xT"], b.times(1))
                    normalise(0, b, xn, x_sb, xn_done)
                if stage == "w":
                    split_lo(k)
                if stage in ("xS", "oS", "x2S"):
                    product = {"xS": "xT", "oS": "oT", "x2S": "x2T"}[stage]
                    bank = x_bank(product, b)
                    hi, lo = {"xT": (xt_h, xt_l), "oT": (ot_h, ot_l), "x2T": (x2_h, x2_l)}[product]
                    reader, n = {"xT": ("v", 1), "oT": ("wo", 1), "x2T": ("gu", NE)}[product]
                    dve.wait_ge(hi_copied[product], b.times(1, 1))
                    wait(dve, ready[reader], b.times(n))
                    nc.vector.tensor_tensor(lo[:, :, :], bank[:, :].rearrange("p (k s) -> p k s", k=KT),
                                            hi[:, :, :].bitcast(F32), ALU.subtract).then_inc(drained[product], 1)
                if stage in ("qS", "kS"):
                    product, n = ("q", 0) if stage == "qS" else ("k", 1)
                    bank = x_bank(product, b)
                    dve.wait_ge(hi_copied[product], b.times(1, 1))
                    wait(dve, low_done, b.times(2))
                    nc.vector.tensor_tensor(rest[n][:, :, :], bank[:, :].rearrange("p (k s) -> p k s", k=KT),
                                            parts[:, n, :, 0, :], ALU.subtract)\
                        .then_inc(rest_done, 1)
                if stage == "am":
                    if k == 0:
                        wait(dve, m_low, b.times(1))
                    for h in (2 * k, 2 * k + 1):
                        dve.wait_ge(a_ready, b.times(NH, h + 1))
                        nc.vector.tensor_reduce(nmax[:, 0:NC_, h], SA[h % 2][:, 0:SC]
                                                .rearrange("p (c s) -> p c s", s=BS), AX.X, ALU.max, negate=True)\
                            .then_inc(a_max, 1)
                if stage == "o":
                    po = PO[k % 2][:, 0:2 * NC_ * VW].rearrange("p (h c v) -> p h c v", h=2, v=VW)
                    dve.wait_ge(pv_ready, b.times(8, k + 1))
                    wait(dve, inv_done, b.times(8, k))
                    nc.vector.tensor_tensor(lsum[:, :, :], po[:, :, :, HD],
                                            excluded.unsqueeze(1).to_broadcast([P, 2, NC_]), ALU.add)\
                        .then_inc(sum_done, 1)
                    dve.wait_ge(sum_done, b.times(8, k + 1))
                    wait(dve, pv_drained, b.times(8, k))
                    nc.vector.reciprocal(linv[:, :, :], lsum[:, :, :]).then_inc(inv_done, 1)
                    dve.wait_ge(inv_done, b.times(8, k + 1))
                    wait(dve, o_done, b.times(16, 2 * k))
                    for h in range(2):
                        last = nc.vector.tensor_tensor(oblk[:, h, :, :], po[:, h, :, 0:HD],
                                                linv[:, h, :].unsqueeze(2).to_broadcast([P, NC_, HD]), ALU.mult)
                    last.then_inc(pv_drained, 1)
                    dve.wait_ge(pv_drained, b.times(8, k + 1))
                    if k == 0:
                        wait(dve, ready["oT"], b.times(1))
                    for t, c in ((0, slice(NBLK, NC_)), (1, slice(0, NBLK))):
                        nc.vector.tensor_reduce(
                            o_sb[:, t, 2 * HD * k:2 * HD * (k + 1)].rearrange("p (h d) -> p h d", h=2),
                            oblk[:, :, c, :].rearrange("p h c d -> p h d c"), AX.X, ALU.add).then_inc(o_done, 1)
                if stage == "res":
                    bank = x_bank("wo", b)
                    y = x1[b.parity]
                    dve.wait_ge(ready["wo"], b.times(1, 1))
                    dve.wait_ge(xres_loaded, b.times(16, 16))
                    if not (b.trip is None and b.base < 2):
                        dve.wait_ge(out_stored[b.parity], b.pairs(16 * TT, b.parity))
                    for t in range(TT):
                        nc.vector.scalar_tensor_tensor(out=y[:, t, :], in0=bank[:, H * t:H * (t + 1)],
                                                       scalar=norm[:, t:t + 1], in1=xres[:, t, :],
                                                       op0=ALU.mult, op1=ALU.add).then_inc(x1_done, 1)
                    dve.wait_ge(x1_done, b.times(TT, TT))
                    layernorm_stats(1, b, y)
                if stage == "nm":
                    wait(dve, ready["x2T"], b.times(1))
                    normalise(1, b, xn2, x1[b.parity], xn2_done)
                if stage == "top":
                    bank = x_bank("lt", b)
                    dve.wait_ge(ready["lt"], b.times(1, 1))
                    nc.vector.tensor_copy(logit[:, :, :], bank[:, 0:TT * NE].rearrange("p (t e) -> p t e", t=TT))\
                        .then_inc(drained["lt"], 1)
                    dve.wait_ge(drained["lt"], b.times(1, 1))
                    nc.vector.tensor_reduce(lmax[:, :], logit[:, :, :], AX.X, ALU.max).then_inc(lmax_done, 1)
                    dve.wait_ge(lmax_done, b.times(1, 1))
                    wait(dve, lexp_done, b.times(1))
                    nc.vector.tensor_tensor(ldiff[:, :, :], logit[:, :, :],
                                            lmax[:, :].unsqueeze(2).to_broadcast([P, TT, NE]), ALU.subtract)\
                        .then_inc(ldiff_done, 1)
                    for t in range(TT):
                        mine = logit[:, t, :].unsqueeze(2).to_broadcast([P, NE, NE])
                        other = logit[:, t, :].unsqueeze(1).to_broadcast([P, NE, NE])
                        nc.vector.tensor_tensor(equal[:, t], other, mine, ALU.is_equal).then_inc(cmp_done, 1)
                        nc.vector.tensor_tensor(above[:, t], other, mine, ALU.is_gt).then_inc(cmp_done, 1)
                    dve.wait_ge(cmp_done, b.times(2 * TT, 2 * TT))
                    nc.vector.tensor_tensor(equal[:, :, :, :], equal[:, :, :, :],
                                            before.unsqueeze(1).to_broadcast([P, TT, NE, NE]), ALU.mult)\
                        .then_inc(tied_done, 1)
                    dve.wait_ge(tied_done, b.times(1, 1))
                    nc.vector.tensor_tensor(beats[:, :, :, :], equal[:, :, :, :], above[:, :, :, :], ALU.add)\
                        .then_inc(beats_done, 1)
                    dve.wait_ge(beats_done, b.times(1, 1))
                    nc.vector.tensor_reduce(rank[:, :, :], beats[:, :, :, :], AX.X, ALU.add).then_inc(rank_done, 1)
                    dve.wait_ge(rank_done, b.times(1, 1))
                    dve.wait_ge(lexp_done, b.times(1, 1))
                    nc.vector.scalar_tensor_tensor(out=picked[:, :, :], in0=rank[:, :, :], scalar=1.5,
                                                   in1=lexp[:, :, :], op0=ALU.is_lt, op1=ALU.mult)\
                        .then_inc(picked_done, 1)
                    dve.wait_ge(picked_done, b.times(1, 1))
                    nc.vector.tensor_reduce(psumm[:, :], picked[:, :, :], AX.X, ALU.add).then_inc(psumm_done, 1)
                    dve.wait_ge(psumm_done, b.times(1, 1))
                    wait(dve, s_low, b.times(1))
                    wait(dve, s_rest, b.times(1))
                    nc.vector.reciprocal(pinv[:, :], psumm[:, :]).then_inc(pinv_done, 1)
                    dve.wait_ge(pinv_done, b.times(1, 1))
                    nc.vector.tensor_tensor(score[:, :, :], picked[:, :, :],
                                            pinv[:, :].unsqueeze(2).to_broadcast([P, TT, NE]), ALU.mult)\
                        .then_inc(score_done, 1)
                if stage == "gd":
                    bank = x_bank("gu", b, k)
                    dve.wait_ge(tanh_done, b.times(NE, k + 1))
                    dve.wait_ge(drained["sb"], b.times(4, k // 2 + 1))
                    if k >= 2 or not (b.trip is None and b.base == 0):
                        dve.wait_ge(hid_done, b.times(NE, k - 1))
                    nc.vector.scalar_tensor_tensor(out=gsil[k % 2][:, :], in0=th[k % 2][:, :], scalar=1.0,
                                                   in1=bank[:, 0:S], op0=ALU.add, op1=ALU.mult).then_inc(act_done, 1)
                    last = nc.vector.scalar_tensor_tensor(out=ups[k % 2][:, :], in0=bank[:, S:2 * S], scalar=0.5,
                                                          in1=sbc[:, k, :], op0=ALU.mult, op1=ALU.mult)
                    last.then_inc(drained["gu"], 1)
                if stage == "dx":
                    bank = x_bank("dn", b, k)
                    dve.wait_ge(ready["dn"], b.times(TT, k + 1))
                    dve.wait_ge(x1_done, b.times(TT, TT))
                    nc.vector.tensor_tensor(x1[b.parity][:, k, :], bank[:, 0:H], x1[b.parity][:, k, :], ALU.add)\
                        .then_inc(drained["dn"], 1)

        @block.tensor
        def _(pe):
            def three_products(dst, lhs, rhs, ks, first, last):
                todo = [(k, p) for k in ks for p in ((0, 0), (0, 1), (1, 0))]
                for n, (k, (a, c)) in enumerate(todo):
                    ins = pe.matmul(dst, lhs(a, k), rhs(c, k), start=first and n == 0,
                                    stop=last and n == len(todo) - 1)
                return ins

            pe.wait_ge(consts_loaded, 16)
            for stage, b, k in walk(pe, PE_ORDER):
                if stage in SHARED:
                    bank = x_bank(stage, b, k)
                    if (stage, b.base, k) in BEFORE:
                        s, base, idx = BEFORE[stage, b.base, k]
                        pb_ = Seq(b.trip, base)
                        if s in ("q", "k"):
                            pe.wait_ge(rest_done, pb_.times(2, 1 if s == "q" else 2))
                        elif s == "wo":
                            pe.wait_ge(x1_done, pb_.times(TT, TT))
                        else:
                            pe.wait_ge(drained[s], pb_.times(PER.get(s, 1), idx + 1))
                if stage in ("xT", "oT", "x2T"):
                    src, done, n = {"xT": (xn, xn_done, TT), "oT": (o_sb, o_done, 16), "x2T": (xn2, xn2_done, TT)}[stage]
                    pe.wait_ge(done, b.times(n, n))
                    for kt in range(KT):
                        for t in range(TT):
                            last = pe.transpose(bank[:, S * kt + P * t:S * kt + P * (t + 1)],
                                                src[:, t, P * kt:P * (kt + 1)], ident_f)
                    last.then_inc(ready[stage], 1)
                if stage in ("q", "k"):
                    n = 0 if stage == "q" else 1
                    if b.trip is None and b.base == 0:
                        pe.wait_ge(lo_split, N_QKV)
                    pe.wait_ge(drained["xT"], b.times(1, 1))
                    for t in range(KT):
                        cols = slice(H * n + P * t, H * n + P * (t + 1))
                        last = three_products(bank[:, S * t:S * (t + 1)], lambda a, kt: (wqkv_h, wqkv_l)[a][:, kt, cols],
                                              lambda a, kt: (xt_h, xt_l)[a][:, kt, :], range(KT), True, True)
                    last.then_inc(ready[stage], 1)
                if stage == "v":
                    if b.trip is None and b.base == 0:
                        pe.wait_ge(lo_split, N_QKV)
                    pe.wait_ge(drained["xT"], b.times(1, 1))
                    for t in range(TT):
                        last = three_products(bank[:, H * t:H * (t + 1)],
                                              lambda a, kt: (xt_h, xt_l)[a][:, kt, P * t:P * (t + 1)],
                                              lambda a, kt: (wqkv_h, wqkv_l)[a][:, kt, 2 * H:3 * H], range(KT), True, True)
                    last.then_inc(ready["v"], 1)
                if stage == "A":
                    q, key = QS[b.parity], KS[b.parity]
                    if k == 0:
                        if b.trip is None and b.base == 0:
                            pe.wait_ge(tables_loaded, 16)
                        pe.wait_ge(stack_loaded[b.parity], b.pairs(16 * 12, 16 * 12))
                    for h in (2 * k, 2 * k + 1):
                        if h >= 2 or not (b.trip is None and b.base == 0):
                            pe.wait_ge(a_max, b.times(NH, h - 1))
                        bank = SA[h % 2]
                        pe.matmul(bank[:, 0:S], q[0:DOT_ROWS, h, P:S], key[0:DOT_ROWS, h, :], start=True, stop=False)
                        pe.matmul(bank[:, P:S], ident_b, mask_a, start=False, stop=True)
                        pe.matmul(bank[:, S:SC], q[0:DOT_ROWS, h, 0:P], key[0:DOT_ROWS, h, 0:P], start=True, stop=False)
                        pe.matmul(bank[:, S:SC], ident_b, mask_a, start=False, stop=True)\
                            .then_inc(a_ready, 1)
                if stage == "mT":
                    pe.wait_ge(m_low, b.times(1, 1))
                    bb = bank[:, :].bitcast(BF16)
                    for p in range(NPART):
                        for t, c in ((0, NBLK), (1, 0)):
                            last = pe.transpose(bb[:, S * p + P * t:S * p + P * (t + 1)],
                                                mpart[:, p, NH * c:NH * (c + NBLK)], ident_b)
                    last.then_inc(ready["mT"], 1)
                if stage == "B":
                    q, key = QS[b.parity], KS[b.parity]
                    if k == 0:
                        pe.wait_ge(m_loaded, b.times(16, 16))
                        if b.trip is None and b.base == 0:
                            pe.wait_ge(blocks_loaded, 32)
                    for h in (2 * k, 2 * k + 1):
                        if h >= 2 or not (b.trip is None and b.base == 0):
                            pe.wait_ge(exp_done, b.times(NH, h - 1))
                        bank = SB[h % 2]
                        pe.matmul(bank[:, 0:S], key[:, h, 0:P], q[:, h, :], start=True, stop=False)
                        pe.matmul(bank[:, 0:P], ident_b, mask_b, start=False, stop=True)
                        pe.matmul(bank[:, S:SC], key[:, h, P:S], q[:, h, P:S], start=True, stop=False)
                        pe.matmul(bank[:, S:SC], ident_b, mask_b, start=False, stop=True)\
                            .then_inc(b_ready, 1)
                if stage == "PV":
                    if k == 0:
                        pe.wait_ge(drained["v"], b.times(1, 1))
                    pe.wait_ge(exp_done, b.times(NH, 2 * k + 2))
                    if k >= 2 or not (b.trip is None and b.base == 0):
                        pe.wait_ge(pv_drained, b.times(8, k - 1))
                    for n in range(2):
                        v = VB[b.parity]
                        o = PO[k % 2][:, NC_ * VW * n:NC_ * VW * (n + 1)]
                        for dst, src, t in ((0, P, 0), (PW, S, 1), (2 * PW, 0, 0)):
                            last = pe.matmul(o[:, dst:dst + PW], PT[k % 2][:, n, src:src + P], v[:, t, 2 * k + n, :],
                                             start=True, stop=True)
                    last.then_inc(pv_ready, 1)
                if stage == "wo":
                    if b.trip is None and b.base == 0:
                        pe.wait_ge(lo_split, N_WO)
                    pe.wait_ge(drained["oT"], b.times(1, 1))
                    for t in range(TT):
                        last = three_products(bank[:, H * t:H * (t + 1)],
                                              lambda a, kt: (ot_h, ot_l)[a][:, kt, P * t:P * (t + 1)],
                                              lambda a, kt: (wo_h, wo_l)[a][:, kt, :], range(KT), True, True)
                    last.then_inc(ready["wo"], 1)
                if stage == "rt":
                    if b.trip is None and b.base == 0:
                        pe.wait_ge(wr_split, 2)
                    pe.wait_ge(drained["x2T"], b.times(1, 1))
                    for n in range(2 * KT):
                        last = pe.matmul(bank[0:2 * NE, 0:S], wr_parts[:, n // 2, :, :].rearrange("p a e -> p (a e)"),
                                         (x2_h, x2_l)[n % 2][:, n // 2, :], start=(n == 0), stop=(n == 2 * KT - 1))
                    last.then_inc(ready["rt"], 1)
                if stage == "lt":
                    pe.wait_ge(drained["rt"], b.times(1, 1))
                    for t in range(TT):
                        last = pe.matmul(bank[:, NE * t:NE * (t + 1)], lparts[:, P * t:P * (t + 1)], add_parts,
                                         start=True, stop=True)
                    last.then_inc(ready["lt"], 1)
                if stage == "sT":
                    pe.wait_ge(s_low, b.times(1, 1))
                    bb = bank[:, :].bitcast(BF16)
                    for t in range(TT):
                        last = pe.transpose(bb[0:MAX_ROWS, P * t:P * (t + 1)],
                                            spart[:, t, :, :].rearrange("p a e -> p (a e)"), ident_b)
                    last.then_inc(ready["sT"], 1)
                if stage == "sb":
                    if b.trip is None and b.base == 0 and k == 0:
                        pe.wait_ge(sel_loaded, 16)
                    pe.wait_ge(drained["sT"], b.times(1, 1))
                    for n in range(2):
                        last = pe.matmul(bank[:, S * n:S * (n + 1)], sel[:, 2 * k + n, :], st_sb[:, :],
                                         start=True, stop=True)
                    last.then_inc(ready["sb"], 1)
                if stage == "gu":
                    if b.trip is None and b.base == 0 and k == 0:
                        pe.wait_ge(lo_split, N_GU)
                    if k == 0:
                        pe.wait_ge(drained["x2T"], b.times(1, 1))
                    for g in range(2):
                        last = three_products(bank[:, S * g:S * (g + 1)],
                                              lambda a, kt: (wgu_h, wgu_l)[a][:, k, kt, g, :],
                                              lambda a, kt: (x2_h, x2_l)[a][:, kt, :], range(KT), True, True)
                    last.then_inc(ready["gu"], 1)
                if stage == "dn":
                    if b.trip is None and b.base == 0:
                        pe.wait_ge(lo_split, N_DN)
                    pe.wait_ge(hid_lo, b.times(NE, NE))
                    last = three_products(bank[:, 0:H], lambda a, e: (hid_h, hid_l)[a][:, e, P * k:P * (k + 1)],
                                          lambda a, e: (wdn_h, wdn_l)[a][:, e, :], range(NE), True, True)
                    last.then_inc(ready["dn"], 1)


def constants():
    import numpy as np

    c, tab = np.zeros((P, CONSTS), np.float32), np.zeros((P, 3 * P), np.float32)
    p = np.arange(P)
    c[:, 0:P] = np.eye(P)
    blk = p // BS
    own = np.concatenate([np.repeat((BPT + blk)[:, None], NBLK, 1), np.repeat(blk[:, None], BPT, 1)], 1)
    j = np.concatenate([np.arange(NBLK), np.arange(BPT)])[None, :]
    c[:, P:P + NC_] = j > own
    for t in range(TT):
        c[:, P + NC_ + t] = 1.0 / (BPT * t + blk + 1 + 1e-6)
    e = np.arange(NE)
    c[:, 152:216] = (e[None, :] < e[:, None]).reshape(-1)[None, :]
    q, k = p[:, None], p[None, :]
    c[0:2 * NE, 216:CONSTS] = np.arange(2 * NE)[:, None] % NE == e[None, :]
    tab[:, 0:P] = np.eye(P)
    tab[:, P:2 * P] = np.where((q // BS == k // BS) & (k > q), MASKED, 0.0)
    tab[:, 2 * P:3 * P] = np.where(q > k, MASKED, 0.0)
    r = np.arange(MAX_ROWS)
    i = ((np.arange(S)[None, :] // BS) == (r[:, None] % NBLK)).astype(np.float32)
    s = np.zeros((MAX_ROWS, NE, P), np.float32)
    for n in r:
        s[n, n % NE, :] = 1.0
    return c, *((a.reshape(len(a), -1).view(np.uint32) >> 16).astype(np.uint16).view(np.float32) for a in (tab, i, s))


def kernel(L0_attn_hidden_states, L0_attn_Wq, L0_attn_Wk, L0_attn_Wv, L0_attn_Wo, L0_ffn_router_gate,
           L0_ffn_expert_gate_up, L0_ffn_expert_down):
    import numpy as np
    import concourse.bacc as bacc
    from concourse.bass_utils import run_bass_kernel_spmd

    def on_partitions(w):
        return w.T.reshape(KT, P, -1).transpose(1, 0, 2)

    wqkv = np.concatenate([on_partitions(np.asarray(w)) for w in (L0_attn_Wq, L0_attn_Wk, L0_attn_Wv)], 2)
    wgu = np.asarray(L0_ffn_expert_gate_up).reshape(NE, KT, P, NI, 2).transpose(2, 0, 1, 4, 3)
    c, t, i, s = constants()
    arrays = {
        "x": np.asarray(L0_attn_hidden_states), "wqkv": wqkv, "wo": on_partitions(np.asarray(L0_attn_Wo)),
        "wr": on_partitions(np.asarray(L0_ffn_router_gate)), "wgu": wgu,
        "wdn": np.asarray(L0_ffn_expert_down).transpose(1, 0, 2), "consts": c,
        "tables": t, "blocks": i, "selc": s,
    }
    arrays = {n: np.ascontiguousarray(a) for n, a in arrays.items()}
    nc = bacc.Bacc("TRN2", target_bir_lowering=False, num_devices=1)
    args = {n: nc.dram_tensor(n, a.shape, F32, kind="ExternalInput").ap() for n, a in arrays.items()}
    args["out"] = nc.dram_tensor("out", (NB, S, H), F32, kind="ExternalOutput").ap()
    args["parts_d"] = nc.dram_tensor("parts_d", (2, 2, H, NPART, S), BF16, kind="Internal").ap()
    args["max_d"] = nc.dram_tensor("max_d", (NPART, NBLK, NH, S), BF16, kind="Internal").ap()
    preln_block_attention_moe(nc, **args)
    r = run_bass_kernel_spmd(nc, [arrays], core_ids=[0])
    return r.results[0]["out"]
```
